# Optimizing a Trainium2 kernel written in Bass

```python
import numpy as np
import jax
import jax.numpy as jnp

def _softmax(x, axis=-1):
    return jax.nn.softmax(x, axis=axis)
def _gelu(x):
    return jax.nn.gelu(x, approximate=True)
def _silu(x):
    return jax.nn.silu(x)
def _sigmoid(x):
    return jax.nn.sigmoid(x)
def _layernorm(x, axis=-1, eps=1e-5):
    m = jnp.mean(x, axis=axis, keepdims=True)
    v = jnp.var(x, axis=axis, keepdims=True)
    return (x - m) / jnp.sqrt(v + eps)
def _scatter_add(tgt, idx, src, axis=0):
    return tgt.at[idx].add(src)
def _segment_sum(src, seg, n):
    return jax.ops.segment_sum(src, seg, n)

kernel_name = 'mk_conv_seq_d1_conv_nchw256_dc359e'

def setup_inputs(seed: int = 0):
    np.random.seed(seed)
    _w = jnp.asarray
    def _rec_inputs():
        import jax
        import jax.numpy as jnp
        _gk = jax.random.key(seed)
        x = -0.0003929 + 0.9999 * jax.random.normal(jax.random.fold_in(_gk, 1), (16, 256, 64, 64), jnp.float32)
        return x
    x = _rec_inputs()
    def _L0_conv_setup():
        import jax, jax.numpy as jnp
        import numpy as np
        E, K = (4, 2)

        def dwconv3(x, w):
            return jax.lax.conv_general_dilated(x, w, (1, 1), 'SAME', feature_group_count=x.shape[1], dimension_numbers=('NCHW', 'OIHW', 'NCHW'))

        def conv1x1(x, w):
            return jnp.einsum('bchw,oc->bohw', x, w)
        key = jax.random.key(seed)
        ks = jax.random.split(key, 24)
        B, C, H, W = (16, 256, 64, 64)
        Cs, Cd, OS, OD, R = (128, 128, 128, 128, 16)
        Ce = 2 * Cd

        def n(k, shape, s=0.05):
            return jax.random.normal(k, shape, dtype=jnp.float32) * s

        def u(k, shape):
            return jax.random.uniform(k, shape, dtype=jnp.float32, minval=0.5, maxval=1.5)
        return {'x': jax.random.normal(ks[0], (B, C, H, W), dtype=jnp.float32), 'sw_dw': n(ks[1], (Cs, 1, 3, 3), 0.2), 'sbn1_s': u(ks[2], (Cs,)), 'sbn1_b': n(ks[3], (Cs,), 0.1), 'sw_pw': n(ks[4], (OS, Cs), 0.1), 'sbn2_s': u(ks[5], (OS,)), 'sbn2_b': n(ks[6], (OS,), 0.1), 'rw1': n(ks[7], (R, Cd), 0.1), 'rb1': jnp.zeros((R,), jnp.float32), 'rw2': n(ks[8], (E, R), 0.1), 'rb2': jnp.zeros((E,), jnp.float32), 'ew_exp': n(ks[9], (E, Ce, Cd), 0.1), 'e1s': u(ks[10], (E, Ce)), 'e1b': n(ks[11], (E, Ce), 0.1), 'ew_dw': n(ks[12], (E, Ce, 1, 3, 3), 0.2), 'e2s': u(ks[13], (E, Ce)), 'e2b': n(ks[14], (E, Ce), 0.1), 'ew_proj': n(ks[15], (E, OD, Ce), 0.1), 'e3s': u(ks[16], (E, OD)), 'e3b': n(ks[17], (E, OD), 0.1), 'pw': n(ks[18], (C, C), 0.1), 'bn_s': u(ks[19], (C,)), 'bn_b': n(ks[20], (C,), 0.1)}
    _L0_conv_all = _L0_conv_setup()
    _L0_conv_in = {k: v for k, v in _L0_conv_all.items() if k in ('sw_dw', 'sbn1_s', 'sbn1_b', 'sw_pw', 'sbn2_s', 'sbn2_b', 'rw1', 'rb1', 'rw2', 'rb2', 'ew_exp', 'e1s', 'e1b', 'ew_dw', 'e2s', 'e2b', 'ew_proj', 'e3s', 'e3b', 'pw', 'bn_s', 'bn_b', )}
    del _L0_conv_all

    return {
        "x": x,
        "L0_conv_sw_dw": _L0_conv_in["sw_dw"],
        "L0_conv_sbn1_s": _L0_conv_in["sbn1_s"],
        "L0_conv_sbn1_b": _L0_conv_in["sbn1_b"],
        "L0_conv_sw_pw": _L0_conv_in["sw_pw"],
        "L0_conv_sbn2_s": _L0_conv_in["sbn2_s"],
        "L0_conv_sbn2_b": _L0_conv_in["sbn2_b"],
        "L0_conv_rw1": _L0_conv_in["rw1"],
        "L0_conv_rb1": _L0_conv_in["rb1"],
        "L0_conv_rw2": _L0_conv_in["rw2"],
        "L0_conv_rb2": _L0_conv_in["rb2"],
        "L0_conv_ew_exp": _L0_conv_in["ew_exp"],
        "L0_conv_e1s": _L0_conv_in["e1s"],
        "L0_conv_e1b": _L0_conv_in["e1b"],
        "L0_conv_ew_dw": _L0_conv_in["ew_dw"],
        "L0_conv_e2s": _L0_conv_in["e2s"],
        "L0_conv_e2b": _L0_conv_in["e2b"],
        "L0_conv_ew_proj": _L0_conv_in["ew_proj"],
        "L0_conv_e3s": _L0_conv_in["e3s"],
        "L0_conv_e3b": _L0_conv_in["e3b"],
        "L0_conv_pw": _L0_conv_in["pw"],
        "L0_conv_bn_s": _L0_conv_in["bn_s"],
        "L0_conv_bn_b": _L0_conv_in["bn_b"],
    }

def reference(x, L0_conv_sw_dw, L0_conv_sbn1_s, L0_conv_sbn1_b, L0_conv_sw_pw, L0_conv_sbn2_s, L0_conv_sbn2_b, L0_conv_rw1, L0_conv_rb1, L0_conv_rw2, L0_conv_rb2, L0_conv_ew_exp, L0_conv_e1s, L0_conv_e1b, L0_conv_ew_dw, L0_conv_e2s, L0_conv_e2b, L0_conv_ew_proj, L0_conv_e3s, L0_conv_e3b, L0_conv_pw, L0_conv_bn_s, L0_conv_bn_b):
    import jax
    import jax.numpy as jnp
    def _L0_conv_ref(x, sw_dw, sbn1_s, sbn1_b, sw_pw, sbn2_s, sbn2_b, rw1, rb1, rw2, rb2, ew_exp, e1s, e1b, ew_dw, e2s, e2b, ew_proj, e3s, e3b, pw, bn_s, bn_b):
        import jax, jax.numpy as jnp
        import numpy as np
        E, K = (4, 2)

        def dwconv3(x, w):
            return jax.lax.conv_general_dilated(x, w, (1, 1), 'SAME', feature_group_count=x.shape[1], dimension_numbers=('NCHW', 'OIHW', 'NCHW'))

        def conv1x1(x, w):
            return jnp.einsum('bchw,oc->bohw', x, w)
        Cs = sw_dw.shape[0]
        x_s, x_d = (x[:, :Cs], x[:, Cs:])
        bc = lambda v: v[None, :, None, None]
        h = jax.nn.silu(dwconv3(x_s, sw_dw) * bc(sbn1_s) + bc(sbn1_b))
        out_s = jax.nn.silu(conv1x1(h, sw_pw) * bc(sbn2_s) + bc(sbn2_b))
        g = jnp.mean(x_d, axis=(2, 3))
        g = jax.nn.silu(g @ rw1.T + rb1)
        logits = g @ rw2.T + rb2
        probs = jax.nn.softmax(logits, axis=-1)
        topw, topi = jax.lax.top_k(probs, K)
        gate = jnp.sum(jax.nn.one_hot(topi, probs.shape[-1], dtype=x.dtype) * topw[..., None], axis=1)

        def expert(we, s1, b1, wd, s2, b2, wp, s3, b3):
            h = jax.nn.silu(conv1x1(x_d, we) * bc(s1) + bc(b1))
            h = jax.nn.silu(dwconv3(h, wd) * bc(s2) + bc(b2))
            h = conv1x1(h, wp) * bc(s3) + bc(b3)
            return h + x_d
        eouts = jax.vmap(expert)(ew_exp, e1s, e1b, ew_dw, e2s, e2b, ew_proj, e3s, e3b)
        out_d = jnp.einsum('ebchw,be->bchw', eouts, gate)
        out = conv1x1(jnp.concatenate([out_s, out_d], axis=1), pw)
        out = out * bc(bn_s) + bc(bn_b)
        return out + x

    def _gn(v, G=32, eps=1e-5):
        B_, C_, H_, W_ = v.shape
        g = v.reshape(B_, G, C_ // G, H_, W_)
        m = jnp.mean(g, axis=(2, 3, 4), keepdims=True)
        s = jnp.var(g, axis=(2, 3, 4), keepdims=True)
        return ((g - m) / jnp.sqrt(s + eps)).reshape(v.shape)

    def _ln_c(v, eps=1e-6):
        m = jnp.mean(v, axis=1, keepdims=True)
        s = jnp.var(v, axis=1, keepdims=True)
        return (v - m) / jnp.sqrt(s + eps)

    def _ln_t(v, eps=1e-5):
        m = jnp.mean(v, axis=-1, keepdims=True)
        s = jnp.var(v, axis=-1, keepdims=True)
        return (v - m) / jnp.sqrt(s + eps)

    def _to_tokens(v):
        B_, C_, H_, W_ = v.shape
        return v.reshape(B_, C_, H_ * W_).transpose(0, 2, 1)
    def _from_tokens(t, like):
        B_, C_, H_, W_ = like.shape
        return t.transpose(0, 2, 1).reshape(B_, C_, H_, W_)

    x = _L0_conv_ref(x, L0_conv_sw_dw, L0_conv_sbn1_s, L0_conv_sbn1_b, L0_conv_sw_pw, L0_conv_sbn2_s, L0_conv_sbn2_b, L0_conv_rw1, L0_conv_rb1, L0_conv_rw2, L0_conv_rb2, L0_conv_ew_exp, L0_conv_e1s, L0_conv_e1b, L0_conv_ew_dw, L0_conv_e2s, L0_conv_e2b, L0_conv_ew_proj, L0_conv_e3s, L0_conv_e3b, L0_conv_pw, L0_conv_bn_s, L0_conv_bn_b)
    return x


_drawn_inputs = setup_inputs


def setup_inputs(seed=0):
    import zlib

    import numpy as np

    out = dict(_drawn_inputs(seed))
    spreads = {'L0_conv_rb1': (0.0, 0.8), 'L0_conv_rb2': (0.0, 0.29)}
    factors = {'L0_conv_rw1': 23.155, 'L0_conv_rw2': 6.537, 'L0_conv_e1b': 4.091}
    for name, (base, spread) in spreads.items():
        noise = np.random.default_rng([zlib.crc32(name.encode()), seed]).standard_normal(out[name].shape)
        drawn = base * np.exp(spread * noise) if base else spread * noise
        out[name] = jnp.asarray(drawn.astype(out[name].dtype))
    for name, factor in factors.items():
        out[name] = (out[name] * factor).astype(out[name].dtype)
    return out
```

```python
from contextlib import ExitStack

import numpy as np

import concourse.bass as bass
from concourse import mybir

F32 = mybir.dt.float32
BF16 = mybir.dt.bfloat16
I32 = mybir.dt.int32
ALU = mybir.AluOpType
ACT = mybir.ActivationFunctionType
AX_X = mybir.AxisListType.X

P = 128
B, C, H, W = 16, 256, 64, 64
E, K, R = 4, 2, 16
CHUNKS = 4
ROWS = H // CHUNKS
PX = ROWS * W
HALF = PX // 2
BLOCKS = 4
STEPS = B * CHUNKS
PAIR = 2 * CHUNKS
SLOTS = 3
GROUPS = P // 32

X_EXP = 0
X_PROJ = X_EXP + 256
X_DW = X_PROJ + 256
X_S1, X_B1 = X_DW + 18, X_DW + 20
X_S2, X_B2 = X_DW + 22, X_DW + 24
X_S3 = X_DW + 26
X_LEN = X_S3 + 128

S_SPW = 0
S_PW = S_SPW + 128
S_BNS = S_PW + 512
S_BNB = S_BNS + 256
S_SBN = S_BNB + 2
S_RW1 = S_SBN + 4
S_RW2 = S_RW1 + R
S_RB1 = S_RW2 + E
S_RB2 = S_RB1 + 1
S_B3 = S_RB2 + E
S_CONV = S_B3 + E
S_EYE = S_CONV + GROUPS * 3
S_TRI = S_EYE + 32
S_IOTA = S_TRI + E * E
S_LEN = S_IOTA + E

POOL_TAPS = [(0, 0), (0, -1), (0, 1), (-1, -1)]
FULL_BELOW = [(1, 0), (-1, 0), (-1, 1), (1, -1), (1, 1)]
FULL_ABOVE = [(-1, 0), (1, 0), (-1, 1), (1, -1), (1, 1)]
NP, NV = len(POOL_TAPS), len(FULL_BELOW)


def vector_taps(c):
    return FULL_ABOVE if c == CHUNKS - 1 else FULL_BELOW


def tap_index(dy, dx):
    return 3 * (dy + 1) + dx + 1


def region(c, dy, dx):
    r0, r1 = max(ROWS * c, -dy), min(ROWS * (c + 1), H - dy)
    x0, x1 = max(0, -dx), W - max(0, dx)
    return r0, r1, x0, x1


def router_step(k):
    return k % CHUNKS == 1 and 0 < k < STEPS - CHUNKS


def plan_psum():
    order = [("bias", 0, 0), ("gate1", -1, 0), ("gate2", -1, 0)]
    for k in range(-2, STEPS + 1):
        order += groups_of(k)
    return {g: (n % 2, order[n - 2] if n >= 2 else None) for n, g in enumerate(order)}


def groups_of(k):
    prev, cur, nxt = 1 <= k, 0 <= k < STEPS, k + 2 < STEPS
    out = []
    if prev:
        out.append(("proj", k - 1, 0))
    if nxt:
        out.append(("expand", k + 2, 0))
    if prev:
        out.append(("final", k - 1, 0))
    if nxt:
        out += [("expand", k + 2, 1), ("expand", k + 2, 2)]
    if router_step(k):
        out.append(("gate1", k // CHUNKS, 0))
    if cur:
        out.append(("sconv", k, 0))
    if prev:
        out.append(("final", k - 1, 1))
    if router_step(k):
        out.append(("gate2", k // CHUNKS, 0))
    if nxt:
        out.append(("expand", k + 2, 3))
    if cur:
        out.append(("spw", k, 0))
    return out


def moe_conv_kernel(nc, x, experts, shared, zeros, out):
    with ExitStack() as ctx:
        def sb(name, shape, dt=F32):
            return ctx.enter_context(nc.sbuf_tensor(name, [P, *shape], dt))

        def sem(name):
            return ctx.enter_context(nc.semaphore(name))

        x_d = sb("x_d", [2, H, W])
        x_res = sb("x_res", [2, ROWS, W])
        x_slot = sb("x_slot", [GROUPS, ROWS, W])
        h = sb("h", [BLOCKS, H, W])
        part_sum = sb("part_sum", [BLOCKS, ROWS, W])
        prod = sb("prod", [NP - 1, ROWS, W])
        h2 = sb("h2", [BLOCKS, PX])
        h2s = sb("h2s", [PX])
        out_s = sb("out_s", [PX])
        out_d = sb("out_d", [PX])
        sel = sb("sel", [2, K, X_LEN])
        proj_w = sb("proj_w", [2, K, 256])
        stat = sb("stat", [S_LEN])
        conv_w = sb("conv_w", [GROUPS * 3, 32])
        pw_s = sb("pw_s", [2, 256])
        b3_out = sb("b3_out", [2, E])
        junk = sb("junk", [PX], BF16)
        xsum = sb("xsum", [CHUNKS])
        gate_h = sb("gate_h", [P])
        logit = sb("logit", [E])
        lmax = sb("lmax", [1])
        zed = sb("zed", [E])
        zsilu = sb("zsilu", [E])
        above = sb("above", [E, E])
        equal = sb("equal", [E, E])
        rank = sb("rank", [E])
        tmp = sb("tmp", [E])
        idx_f = sb("idx_f", [K])
        idx = sb("idx", [K], I32)
        den = sb("den", [E])
        prob = sb("prob", [E])
        psumz = sb("psumz", [1])
        gate = sb("gate", [2, K])
        gate_all = sb("gate_all", [E])
        gate_sum = sb("gate_sum", [2, 1])
        fb_terms = sb("fb_terms", [2, E])
        fb_sum = sb("fb_sum", [2])
        fbias = sb("fbias", [2, 2])

        acc = [ctx.enter_context(nc.psum_tensor(f"acc{s}", [P, ROWS, W], F32)) for s in range(2)]
        mm = [ctx.enter_context(nc.psum_tensor(f"mm{s}", [P, PX], F32)) for s in range(2)]

        rate = {}

        def counter(name, per_pair):
            s = sem(name)
            rate[s.name] = per_pair
            return s

        stat_in = sem("stat_in")
        sp_passed = sem("sp_passed")
        setup = sem("setup")
        pe_bias = sem("pe_bias")
        xd_in = [[counter(f"xd_in{p}{c}", 16) for c in range(CHUNKS)] for p in range(2)]
        xres_in = [counter(f"xres_in{s}", 16 * PAIR // 2) for s in range(2)]
        xslot_in = counter("xslot_in", 16 * 14 * 2)
        sel_in = [counter(f"sel_in{p}", 16 * K) for p in range(2)]
        st_d = [[counter(f"st_d{p}{c}", 16) for c in range(CHUNKS)] for p in range(2)]
        st_s = [counter(f"st_s{s}", 16 * PAIR // 2) for s in range(2)]
        pe_expand = counter("pe_expand", BLOCKS * PAIR)
        pe_sconv = counter("pe_sconv", PAIR)
        pe_spw = counter("pe_spw", PAIR)
        pe_proj = counter("pe_proj", PAIR)
        pe_final = counter("pe_final", 2 * PAIR)
        pe_gate1 = counter("pe_gate1", 2)
        pe_gate2 = counter("pe_gate2", 2)
        act_h = counter("act_h", BLOCKS * PAIR)
        act_prod = counter("act_prod", NP * BLOCKS * PAIR)
        act_h2 = counter("act_h2", BLOCKS * PAIR)
        act_h2s = counter("act_h2s", PAIR)
        act_outs = counter("act_outs", PAIR)
        act_sum = counter("act_sum", CHUNKS * 2)
        act_gate = counter("act_gate", 2)
        act_zsilu = counter("act_zsilu", 2)
        pool_add = counter("pool_add", (NP - 1) * BLOCKS * PAIR)
        dve_tap = counter("dve_tap", NV * BLOCKS * PAIR)
        dve_outd = counter("dve_outd", PAIR)
        dve_out = counter("dve_out", 2 * PAIR)
        N_CHOOSE, N_GATE = 11, 13
        dve_choose = counter("dve_choose", 2 * N_CHOOSE)
        dve_gate = counter("dve_gate", 2 * N_GATE)

        def due(s, value, lap):
            return value if lap is None else lap * rate[s.name] + value

        def image(k, lap):
            i = k // CHUNKS
            return i if lap is None else i + 2 * lap

        def run(eng, step, first, last):
            for k in range(first, PAIR):
                step(k, None)
            with eng.Fori(0, STEPS // PAIR - 2) as lap:
                for k in range(PAIR, 2 * PAIR):
                    step(k, lap)
            for k in range(STEPS - PAIR, last):
                step(k, None)

        def expands(k, b): return BLOCKS * k + b + 1
        def prods(k, b, n): return NP * (BLOCKS * k + b) + n + 1
        def adds(k, b, n): return (NP - 1) * (BLOCKS * k + b) + n + 1
        def h2s_of(k, b): return BLOCKS * k + b + 1
        def taps(k, b, t): return 2 * NV * (2 * k + b // 2) + 2 * t + b % 2 + 1
        def finals(k, m): return 2 * k + m + 1
        def xd_loads(k): return 16 * (k // PAIR + 1)
        def xres_loads(k): return 16 * (k // 2 + 1)
        def xslot_loads(k): return 16 * (14 * (k // CHUNKS) + (4, 7, 10, 14)[k % CHUNKS])

        plan = plan_psum()
        drain = {
            "bias": lambda k, n: (setup, 3),
            "gate1": lambda k, n: (act_gate, k + 2),
            "gate2": lambda k, n: (dve_choose, N_CHOOSE * (k + 1) + 1),
            "proj": lambda k, n: (dve_outd, k + 1),
            "final": lambda k, n: (dve_out, finals(k, n)),
            "expand": lambda k, n: (act_h, expands(k, n)),
            "sconv": lambda k, n: (act_h2s, k + 1),
            "spw": lambda k, n: (act_outs, k + 1),
        }

        def weights(par, slot, col, n=1):
            return sel[:, par, slot, col:col + n]

        block = ctx.enter_context(nc.Block())

        @block.sync
        def _(sp):
            def load_xd(i_static, c, i):
                sp.dma_start(x_d[:, i_static % 2, ROWS * c:ROWS * (c + 1), :],
                             x[i, P:, ROWS * c:ROWS * (c + 1), :]).then_inc(xd_in[i_static % 2][c], 16)

            def load_res(k, lap):
                c = k % CHUNKS
                sp.dma_start(x_res[:, k % 2], x[image(k, lap), 0:P, ROWS * c:ROWS * (c + 1), :]
                             ).then_inc(xres_in[k % 2], 16)

            def load_slots(k, lap):
                c, i = k % CHUNKS, image(k, lap)
                src = x[i, 0:P].rearrange("(g c) y w -> c g y w", g=GROUPS)
                for j in range(SLOTS):
                    r0, r1, _, _ = region(c, j - 1, 0)
                    part = x_slot[32 * j:32 * (j + 1)]
                    sp.dma_start(part[:, :, r0 - ROWS * c:r1 - ROWS * c, :], src[:, :, r0 + j - 1:r1 + j - 1, :]
                                 ).then_inc(xslot_in, 16)
                    if r1 - r0 < ROWS:
                        edge = 0 if j == 0 else ROWS - 1
                        sp.dma_start(part[:, :, edge, :], zeros).then_inc(xslot_in, 16)

            def fetch_experts(i_static, lap):
                par = i_static % 2
                sp.wait_ge(dve_choose, due(dve_choose, N_CHOOSE * (i_static + 1), lap))
                sp.sem_inc(sp_passed, 1)
                if i_static >= 2:
                    sp.wait_ge(pe_proj, due(pe_proj, CHUNKS * (i_static - 1), lap))
                    sp.sem_inc(sp_passed, 1)
                for s in range(K):
                    e = sp.value_load(idx[0:1, s:s + 1], min_val=0, max_val=E - 1)
                    sp.dma_start(sel[:, par, s, :], experts[bass.ds(e, 1), :, :].rearrange("a p l -> (a p) l")
                                 ).then_inc(sel_in[par], 16)

            def step(k, lap):
                if k % CHUNKS == 2 and router_step(k - 1):
                    fetch_experts(k // CHUNKS + 1, lap)
                c, kp = (k - 1) % CHUNKS, k - 1
                if k >= 1:
                    sp.wait_ge(dve_out, due(dve_out, finals(kp, 0), lap))
                    sp.sem_inc(sp_passed, 1)
                    sp.dma_start(out[image(kp, lap), 0:P, ROWS * c:ROWS * (c + 1), :], x_res[:, kp % 2]
                                 ).then_inc(st_s[kp % 2], 16)
                if k + 1 < STEPS:
                    sp.wait_ge(pe_sconv, due(pe_sconv, k + 1, lap))
                    sp.sem_inc(sp_passed, 1)
                    load_slots(k + 1, lap)
                if k >= 1:
                    par = (kp // CHUNKS) % 2
                    sp.wait_ge(dve_out, due(dve_out, finals(kp, 1), lap))
                    sp.sem_inc(sp_passed, 1)
                    sp.dma_start(out[image(kp, lap), P:, ROWS * c:ROWS * (c + 1), :],
                                 x_d[:, par, ROWS * c:ROWS * (c + 1), :]).then_inc(st_d[par][c], 16)
                    if k + 1 < STEPS:
                        sp.wait_ge(st_s[kp % 2], due(st_s[kp % 2], xres_loads(kp), lap))
                        sp.sem_inc(sp_passed, 1)
                        load_res(k + 1, lap)
                    if kp // CHUNKS + 2 < B:
                        sp.wait_ge(st_d[par][c], due(st_d[par][c], xd_loads(kp), lap))
                        sp.sem_inc(sp_passed, 1)
                        load_xd(kp // CHUNKS + 2, c, image(kp, lap) + 2)

            sp.dma_start(stat[:], shared).then_inc(stat_in, 16)
            for c in range(CHUNKS):
                load_xd(0, c, 0)
            fetch_experts(0, None)
            load_slots(0, None)
            load_res(0, None)
            load_res(1, None)
            for c in range(CHUNKS):
                load_xd(1, c, 1)
            run(sp, step, 0, STEPS + 1)
            for s in range(2):
                sp.wait_ge(st_s[s], 16 * STEPS // 2)
                for c in range(CHUNKS):
                    sp.wait_ge(st_d[s][c], 16 * B // 2)

        @block.gpsimd
        def _(pool):
            def step(k, lap):
                c = k % CHUNKS
                for b in range(BLOCKS):
                    for n in range(1, NP):
                        r0, r1, x0, x1 = region(c, *POOL_TAPS[n])
                        total = part_sum[:, b, r0 - ROWS * c:r1 - ROWS * c, x0:x1]
                        pool.wait_ge(act_prod, due(act_prod, prods(k, b, n), lap))
                        if n > 1:
                            pool.wait_ge(pool_add, due(pool_add, adds(k, b, n - 2), lap))
                        nc.gpsimd.tensor_tensor(total, total, prod[:, n - 1, r0 - ROWS * c:r1 - ROWS * c, x0:x1],
                                                ALU.add).then_inc(pool_add, 1)
            run(pool, step, 0, STEPS)

        @block.scalar
        def _(act):
            def sum_x(i_static, c, lap):
                act.wait_ge(xd_in[i_static % 2][c], due(xd_in[i_static % 2][c], xd_loads(CHUNKS * i_static), lap))
                if i_static >= 1:
                    act.wait_ge(pe_gate1, due(pe_gate1, i_static, lap))
                if i_static >= 1 or c >= 1:
                    act.wait_ge(act_sum, due(act_sum, CHUNKS * i_static + c, lap))
                nc.scalar.activation(junk[:], x_d[:, i_static % 2, ROWS * c:ROWS * (c + 1), :].rearrange("p y w -> p (y w)"),
                                     ACT.Copy, accum_out=xsum[:, c:c + 1]).then_inc(act_sum, 1)

            def router_hidden(i_static, lap):
                buf = plan[("gate1", i_static - 1, 0)][0]
                act.wait_ge(pe_gate1, due(pe_gate1, i_static + 1, lap))
                if i_static >= 1:
                    act.wait_ge(pe_gate2, due(pe_gate2, i_static, lap))
                nc.scalar.activation(gate_h[0:R, :], mm[buf][0:R, 0:P], ACT.Silu, bias=stat[0:R, S_RB1:S_RB1 + 1],
                                     scale=1.0 / (H * W)).then_inc(act_gate, 1)

            def router_silu(i_static, lap):
                act.wait_ge(dve_choose, due(dve_choose, N_CHOOSE * i_static + 3, lap))
                nc.scalar.activation(zsilu[:], zed[:], ACT.Silu).then_inc(act_zsilu, 1)

            def expand_out(k, b, lap):
                c, par = k % CHUNKS, (k // CHUNKS) % 2
                act.wait_ge(pe_expand, due(pe_expand, expands(k, b), lap))
                if k >= 3:
                    act.wait_ge(dve_tap, due(dve_tap, taps(k - 3, b, NV - 1), lap))
                nc.scalar.activation(h[:, b, ROWS * c:ROWS * (c + 1), :].rearrange("p y w -> p (y w)"),
                                     mm[plan[("expand", k, b)][0]][:], ACT.Silu,
                                     bias=weights(par, b // 2, X_B1 + b % 2), scale=weights(par, b // 2, X_S1 + b % 2)
                                     ).then_inc(act_h, 1)

            def product(k, b, n, lap):
                c, par = k % CHUNKS, (k // CHUNKS) % 2
                dy, dx = POOL_TAPS[n]
                r0, r1, x0, x1 = region(c, dy, dx)
                if n == 0:
                    act.wait_ge(act_h, due(act_h, expands(k, b), lap))
                    if k >= 1:
                        act.wait_ge(dve_tap, due(dve_tap, taps(k - 1, b, 0), lap))
                    dst = part_sum[:, b]
                else:
                    if k >= 1 or b >= 1:
                        act.wait_ge(pool_add, due(pool_add, adds(k, b, n - 1) - (NP - 1), lap))
                    dst = prod[:, n - 1]
                nc.scalar.activation(dst[:, r0 - ROWS * c:r1 - ROWS * c, x0:x1], h[:, b, r0 + dy:r1 + dy, x0 + dx:x1 + dx],
                                     ACT.Copy, scale=weights(par, b // 2, X_DW + 9 * (b % 2) + tap_index(dy, dx))
                                     ).then_inc(act_prod, 1)

            def expert_out(k, b, lap):
                par = (k // CHUNKS) % 2
                act.wait_ge(dve_tap, due(dve_tap, taps(k, b, NV - 1), lap))
                if k >= 1:
                    act.wait_ge(pe_proj, due(pe_proj, k, lap))
                nc.scalar.activation(h2[:, b, :], acc[b % 2][:].rearrange("p y w -> p (y w)"), ACT.Silu,
                                     bias=weights(par, b // 2, X_B2 + b % 2), scale=weights(par, b // 2, X_S2 + b % 2)
                                     ).then_inc(act_h2, 1)

            def shared_hidden(k, lap):
                act.wait_ge(pe_sconv, due(pe_sconv, k + 1, lap))
                if k >= 1:
                    act.wait_ge(pe_spw, due(pe_spw, k, lap))
                nc.scalar.activation(h2s[:], mm[plan[("sconv", k, 0)][0]][:], ACT.Silu, bias=stat[:, S_SBN + 1:S_SBN + 2], scale=stat[:, S_SBN:S_SBN + 1]
                                     ).then_inc(act_h2s, 1)

            def shared_out(k, lap):
                act.wait_ge(pe_spw, due(pe_spw, k + 1, lap))
                if k >= 1:
                    act.wait_ge(pe_final, due(pe_final, finals(k - 1, 1), lap))
                nc.scalar.activation(out_s[:], mm[plan[("spw", k, 0)][0]][:], ACT.Silu,
                                     bias=stat[:, S_SBN + 3:S_SBN + 4], scale=stat[:, S_SBN + 2:S_SBN + 3]
                                     ).then_inc(act_outs, 1)

            def step(k, lap):
                prev, cur, nxt, late = 1 <= k, 0 <= k < STEPS, k + 2 < STEPS, -2 < k and k + 1 < STEPS
                ahead = 0 <= k + 1 < STEPS
                def products(when, kk, b, ns):
                    if when:
                        for n in ns:
                            product(kk, b, n, lap)
                if late:
                    expand_out(k + 1, 3, lap)
                products(cur, k, 2, [0, 1])
                if prev:
                    shared_out(k - 1, lap)
                products(cur, k, 2, [2, 3])
                products(cur, k, 3, [0])
                if nxt:
                    expand_out(k + 2, 0, lap)
                products(cur, k, 3, [1, 2])
                if router_step(k):
                    for c in range(CHUNKS):
                        sum_x(k // CHUNKS + 1, c, lap)
                products(cur, k, 3, [3])
                if cur:
                    expert_out(k, 0, lap)
                    expert_out(k, 1, lap)
                if nxt:
                    expand_out(k + 2, 1, lap)
                products(ahead, k + 1, 0, [0, 1])
                if nxt:
                    expand_out(k + 2, 2, lap)
                if router_step(k):
                    router_hidden(k // CHUNKS + 1, lap)
                products(ahead, k + 1, 0, [2, 3])
                products(ahead, k + 1, 1, [0])
                if cur:
                    shared_hidden(k, lap)
                products(ahead, k + 1, 1, [1, 2])
                if cur:
                    expert_out(k, 2, lap)
                products(ahead, k + 1, 1, [3])
                if cur:
                    expert_out(k, 3, lap)
                if router_step(k):
                    router_silu(k // CHUNKS + 1, lap)

            for c in range(CHUNKS):
                sum_x(0, c, None)
            act.wait_ge(stat_in, 16)
            router_hidden(0, None)
            router_silu(0, None)
            act.wait_ge(sel_in[0], 16 * K)
            run(act, step, -2, STEPS + 1)

        @block.vector
        def _(dve):
            def choose(i_static, lap):
                done = N_CHOOSE * i_static
                buf = plan[("gate2", i_static - 1, 0)][0]
                dve.wait_ge(pe_gate2, due(pe_gate2, i_static + 1, lap))
                if i_static >= 1:
                    dve.wait_ge(act_zsilu, due(act_zsilu, i_static, lap))
                nc.vector.tensor_tensor(logit[:], mm[buf][:, 0:E], stat[:, S_RB2:S_RB2 + E], ALU.add).then_inc(dve_choose, 1)
                dve.wait_ge(dve_choose, due(dve_choose, done + 1, lap))
                nc.vector.reduce_max(lmax[:], logit[:], AX_X).then_inc(dve_choose, 1)
                dve.wait_ge(dve_choose, due(dve_choose, done + 2, lap))
                nc.vector.tensor_scalar(zed[:], logit[:], lmax[:], -1.0, ALU.subtract, ALU.add).then_inc(dve_choose, 1)
                by_f = logit[:].unsqueeze(1).broadcast_to([P, E, E])
                by_e = logit[:].unsqueeze(2).broadcast_to([P, E, E])
                nc.vector.tensor_tensor(equal[:], by_f, by_e, ALU.is_equal).then_inc(dve_choose, 1)
                nc.vector.tensor_tensor(above[:], by_f, by_e, ALU.is_gt).then_inc(dve_choose, 1)
                dve.wait_ge(dve_choose, due(dve_choose, done + 4, lap))
                nc.vector.tensor_tensor(equal[:], equal[:], stat[:, S_TRI:S_TRI + E * E].rearrange("p (e f) -> p e f", e=E),
                                        ALU.mult).then_inc(dve_choose, 1)
                dve.wait_ge(dve_choose, due(dve_choose, done + 6, lap))
                nc.vector.tensor_tensor(above[:], above[:], equal[:], ALU.add).then_inc(dve_choose, 1)
                dve.wait_ge(dve_choose, due(dve_choose, done + 7, lap))
                if i_static >= 1:
                    dve.wait_ge(dve_gate, due(dve_gate, N_GATE * i_static, lap))
                nc.vector.reduce_sum(rank[:], above[:], AX_X).then_inc(dve_choose, 1)
                for s in range(K):
                    dve.wait_ge(dve_choose, due(dve_choose, done + 8 + s, lap))
                    nc.vector.scalar_tensor_tensor(tmp[:], rank[:], float(s), stat[:, S_IOTA:S_IOTA + E], ALU.is_equal,
                                                   ALU.mult, accum_out=idx_f[:, s:s + 1]).then_inc(dve_choose, 1)
                dve.wait_ge(dve_choose, due(dve_choose, done + 10, lap))
                nc.vector.tensor_copy(idx[:], idx_f[:]).then_inc(dve_choose, 1)

            def gates(i_static, lap):
                done, par = N_GATE * i_static, i_static % 2
                dve.wait_ge(act_zsilu, due(act_zsilu, i_static + 1, lap))
                nc.vector.tensor_tensor(den[:], zed[:], zsilu[:], ALU.subtract).then_inc(dve_gate, 1)
                dve.wait_ge(dve_gate, due(dve_gate, done + 1, lap))
                nc.vector.reciprocal(den[:], den[:]).then_inc(dve_gate, 1)
                dve.wait_ge(dve_gate, due(dve_gate, done + 2, lap))
                nc.vector.scalar_tensor_tensor(prob[:], zsilu[:], 1.0, den[:], ALU.mult, ALU.mult,
                                               accum_out=psumz[:]).then_inc(dve_gate, 1)
                dve.wait_ge(dve_gate, due(dve_gate, done + 3, lap))
                nc.vector.reciprocal(psumz[:], psumz[:]).then_inc(dve_gate, 1)
                dve.wait_ge(dve_gate, due(dve_gate, done + 4, lap))
                nc.vector.tensor_scalar(prob[:], prob[:], psumz[:], None, ALU.mult).then_inc(dve_gate, 1)
                for s in range(K):
                    dve.wait_ge(dve_gate, due(dve_gate, done + 5 + s, lap))
                    nc.vector.scalar_tensor_tensor(tmp[:], rank[:], float(s), prob[:], ALU.is_equal, ALU.mult,
                                                   accum_out=gate[:, par, s:s + 1]).then_inc(dve_gate, 1)
                dve.wait_ge(dve_gate, due(dve_gate, done + 7, lap))
                nc.vector.scalar_tensor_tensor(gate_all[:], rank[:], float(K), prob[:], ALU.is_lt, ALU.mult,
                                               accum_out=gate_sum[:, par, :]).then_inc(dve_gate, 1)
                dve.wait_ge(dve_gate, due(dve_gate, done + 8, lap))
                nc.vector.tensor_tensor(fb_terms[:], b3_out[:], gate_all[:].unsqueeze(1).broadcast_to([P, 2, E]),
                                        ALU.mult).then_inc(dve_gate, 1)
                dve.wait_ge(dve_gate, due(dve_gate, done + 9, lap))
                nc.vector.reduce_sum(fb_sum[:], fb_terms[:], AX_X).then_inc(dve_gate, 1)
                dve.wait_ge(dve_gate, due(dve_gate, done + 10, lap))
                nc.vector.tensor_tensor(fbias[:, par, :], fb_sum[:], stat[:, S_BNB:S_BNB + 2], ALU.add).then_inc(dve_gate, 1)
                dve.wait_ge(sel_in[par], due(sel_in[par], 16 * K * (i_static // 2 + 1), lap))
                if i_static >= 2:
                    dve.wait_ge(pe_proj, due(pe_proj, CHUNKS * (i_static - 1), lap))
                for s in range(K):
                    nc.vector.scalar_tensor_tensor(
                        proj_w[:, par, s, :].rearrange("p (b o) -> p b o", b=2),
                        weights(par, s, X_PROJ, 256).rearrange("p (b o) -> p b o", b=2), gate[:, par, s:s + 1],
                        weights(par, s, X_S3, P).unsqueeze(1).broadcast_to([P, 2, P]),
                        ALU.mult, ALU.mult).then_inc(dve_gate, 1)

            def tap(k, b, t, lap):
                c, par = k % CHUNKS, (k // CHUNKS) % 2
                dy, dx = vector_taps(c)[t]
                r0, r1, x0, x1 = region(c, dy, dx)
                dst = acc[b % 2][:, r0 - ROWS * c:r1 - ROWS * c, x0:x1]
                if t == 0:
                    dve.wait_ge(pool_add, due(pool_add, adds(k, b, NP - 2), lap))
                    if c < CHUNKS - 1:
                        dve.wait_ge(act_h, due(act_h, expands(k + 1, b), lap))
                    if k >= 1 or b >= 2:
                        dve.wait_ge(act_h2, due(act_h2, h2s_of(k, b) - 2, lap))
                    before = part_sum[:, b]
                else:
                    dve.wait_ge(dve_tap, due(dve_tap, taps(k, b, t - 1), lap))
                    before = dst
                nc.vector.scalar_tensor_tensor(dst, h[:, b, r0 + dy:r1 + dy, x0 + dx:x1 + dx],
                                               weights(par, b // 2, X_DW + 9 * (b % 2) + tap_index(dy, dx)), before,
                                               ALU.mult, ALU.add).then_inc(dve_tap, 1)

            def expert_sum(k, lap):
                c, par = k % CHUNKS, (k // CHUNKS) % 2
                dve.wait_ge(pe_proj, due(pe_proj, k + 1, lap))
                if k >= 1:
                    dve.wait_ge(pe_final, due(pe_final, finals(k - 1, 1), lap))
                dve.wait_ge(xd_in[par][c], due(xd_in[par][c], xd_loads(k), lap))
                nc.vector.scalar_tensor_tensor(out_d[:], x_d[:, par, ROWS * c:ROWS * (c + 1), :].rearrange("p y w -> p (y w)"),
                                               gate_sum[:, par, :], mm[plan[("proj", k, 0)][0]][:],
                                               ALU.mult, ALU.add).then_inc(dve_outd, 1)

            def output(k, m, lap):
                c, par = k % CHUNKS, (k // CHUNKS) % 2
                dve.wait_ge(pe_final, due(pe_final, finals(k, m), lap))
                if m == 0:
                    dve.wait_ge(xres_in[k % 2], due(xres_in[k % 2], xres_loads(k), lap))
                    place = x_res[:, k % 2].rearrange("p y w -> p (y w)")
                else:
                    dve.wait_ge(dve_outd, due(dve_outd, k + 1, lap))
                    place = x_d[:, par, ROWS * c:ROWS * (c + 1), :].rearrange("p y w -> p (y w)")
                nc.vector.scalar_tensor_tensor(place, mm[plan[("final", k, m)][0]][:], fbias[:, par, m:m + 1], place,
                                               ALU.add, ALU.add).then_inc(dve_out, 1)

            def step(k, lap):
                prev, cur = 1 <= k, k < STEPS
                order = [(t, s) for t in range(NV) for s in range(2)]
                if cur:
                    for t, s in order[:6]:
                        tap(k, s, t, lap)
                if prev:
                    expert_sum(k - 1, lap)
                if cur:
                    for t, s in order[6:]:
                        tap(k, s, t, lap)
                if prev:
                    output(k - 1, 0, lap)
                if k % CHUNKS == 2 and router_step(k - 1):
                    gates(k // CHUNKS + 1, lap)
                if cur:
                    for t, s in order:
                        tap(k, 2 + s, t, lap)
                if prev:
                    output(k - 1, 1, lap)
                if router_step(k):
                    choose(k // CHUNKS + 1, lap)

            dve.wait_ge(stat_in, 16)
            nc.vector.tensor_tensor(pw_s[:], stat[:, S_PW:S_PW + 512].rearrange("p (k o) -> p k o", k=2),
                                    stat[:, S_BNS:S_BNS + 256].unsqueeze(1).broadcast_to([P, 2, 256]),
                                    ALU.mult).then_inc(setup, 1)
            nc.vector.tensor_tensor(conv_w[:], stat[:, S_CONV:S_EYE].unsqueeze(2).broadcast_to([P, GROUPS * 3, 32]),
                                    stat[:, S_EYE:S_EYE + 32].unsqueeze(1).broadcast_to([P, GROUPS * 3, 32]),
                                    ALU.mult).then_inc(setup, 1)
            dve.wait_ge(pe_bias, 1)
            nc.vector.tensor_copy(b3_out[:], mm[plan[("bias", 0, 0)][0]][:, 0:2 * E].rearrange("p (m e) -> p m e", m=2)
                                  ).then_inc(setup, 1)
            dve.wait_ge(setup, 3)
            choose(0, None)
            gates(0, None)
            dve.wait_ge(dve_gate, N_GATE)
            run(dve, step, 0, STEPS + 1)

        @block.tensor
        def _(pe):
            def drained(group, lap):
                name, k, n = plan[group][1]
                s, value = drain[name](k, n)
                return s, due(s, value, lap)

            def expand(k, b, lap):
                c, par = k % CHUNKS, (k // CHUNKS) % 2
                ps = mm[plan[("expand", k, b)][0]]
                pe.wait_ge(*drained(("expand", k, b), lap))
                pe.wait_ge(xd_in[par][c], due(xd_in[par][c], xd_loads(k), lap))
                pe.wait_ge(sel_in[par], due(sel_in[par], 16 * K * (k // PAIR + 1), lap))
                for n in range(2):
                    mmul = nc.tensor.matmul(ps[:, HALF * n:HALF * (n + 1)],
                                            weights(par, b // 2, X_EXP + P * (b % 2), P),
                                            x_d[:, par, ROWS * c + ROWS // 2 * n:ROWS * c + ROWS // 2 * (n + 1), :],
                                            start=True, stop=True)
                mmul.then_inc(pe_expand, 1)

            def shared_conv(k, lap):
                ps = mm[plan[("sconv", k, 0)][0]]
                pe.wait_ge(*drained(("sconv", k, 0), lap))
                pe.wait_ge(xslot_in, due(xslot_in, xslot_loads(k), lap))
                rows = ROWS // 2
                for n in range(2):
                    for t, dx in enumerate((0, -1, 1)):
                        x0, x1 = max(0, -dx), W - max(0, dx)
                        for g in range(GROUPS):
                            dst = ps[32 * g:32 * (g + 1), HALF * n:HALF * (n + 1)].rearrange("p (y w) -> p y w", w=W)
                            mmul = nc.tensor.matmul(dst[:, :, x0:x1], conv_w[0:32 * SLOTS, 3 * g + dx + 1, :],
                                                    x_slot[0:32 * SLOTS, g, rows * n:rows * (n + 1), x0 + dx:x1 + dx],
                                                    start=(t == 0), stop=(t == 2), tile_position=(0, 32 * g))
                mmul.then_inc(pe_sconv, 1)

            def shared_pointwise(k, lap):
                ps = mm[plan[("spw", k, 0)][0]]
                pe.wait_ge(*drained(("spw", k, 0), lap))
                pe.wait_ge(act_h2s, due(act_h2s, k + 1, lap))
                for n in range(2):
                    mmul = nc.tensor.matmul(ps[:, HALF * n:HALF * (n + 1)], stat[:, S_SPW:S_SPW + P],
                                            h2s[:, HALF * n:HALF * (n + 1)], start=True, stop=True)
                mmul.then_inc(pe_spw, 1)

            def proj(k, lap):
                par = (k // CHUNKS) % 2
                ps = mm[plan[("proj", k, 0)][0]]
                pe.wait_ge(*drained(("proj", k, 0), lap))
                pe.wait_ge(dve_gate, due(dve_gate, N_GATE * (k // CHUNKS + 1), lap))
                for b in range(BLOCKS):
                    pe.wait_ge(act_h2, due(act_h2, h2s_of(k, b), lap))
                    for n in range(2):
                        mmul = nc.tensor.matmul(ps[:, HALF * n:HALF * (n + 1)],
                                                proj_w[:, par, b // 2, P * (b % 2):P * (b % 2 + 1)],
                                                h2[:, b, HALF * n:HALF * (n + 1)],
                                                start=(b == 0), stop=(b == BLOCKS - 1))
                mmul.then_inc(pe_proj, 1)

            def final(k, m, lap):
                ps = mm[plan[("final", k, m)][0]]
                pe.wait_ge(*drained(("final", k, m), lap))
                pe.wait_ge(act_outs, due(act_outs, k + 1, lap))
                pe.wait_ge(dve_outd, due(dve_outd, k + 1, lap))
                for half, src in enumerate((out_s, out_d)):
                    for n in range(2):
                        mmul = nc.tensor.matmul(ps[:, HALF * n:HALF * (n + 1)], pw_s[:, half, P * m:P * (m + 1)],
                                                src[:, HALF * n:HALF * (n + 1)], start=(half == 0), stop=(half == 1))
                mmul.then_inc(pe_final, 1)

            def router_first(i_static, lap):
                ps = mm[plan[("gate1", i_static - 1, 0)][0]]
                if i_static >= 1:
                    pe.wait_ge(*drained(("gate1", i_static - 1, 0), lap))
                pe.wait_ge(act_sum, due(act_sum, CHUNKS * (i_static + 1), lap))
                for c in range(CHUNKS):
                    mmul = nc.tensor.matmul(ps[0:R, 0:P], stat[:, S_RW1:S_RW1 + R], xsum[:, c:c + 1].broadcast_to([P, P]),
                                            start=(c == 0), stop=(c == CHUNKS - 1))
                mmul.then_inc(pe_gate1, 1)

            def router_second(i_static, lap):
                ps = mm[plan[("gate2", i_static - 1, 0)][0]]
                pe.wait_ge(*drained(("gate2", i_static - 1, 0), lap))
                pe.wait_ge(act_gate, due(act_gate, i_static + 1, lap))
                nc.tensor.matmul(ps[:, 0:E], gate_h[0:R, :], stat[0:R, S_RW2:S_RW2 + E],
                                 start=True, stop=True).then_inc(pe_gate2, 1)

            do = {"proj": proj, "expand": expand, "final": final, "sconv": shared_conv, "spw": shared_pointwise,
                  "gate1": lambda i, lap: router_first(i + 1, lap), "gate2": lambda i, lap: router_second(i + 1, lap)}

            def step(k, lap):
                for name, kk, n in groups_of(k):
                    if name in ("expand", "final"):
                        do[name](kk, n, lap)
                    else:
                        do[name](kk, lap)

            pe.wait_ge(stat_in, 16)
            pe.wait_ge(setup, 2)
            ps = mm[plan[("bias", 0, 0)][0]]
            for m in range(2):
                mmul = nc.tensor.matmul(ps[:, E * m:E * (m + 1)], pw_s[:, 1, P * m:P * (m + 1)], stat[:, S_B3:S_B3 + E],
                                        start=True, stop=True)
            mmul.then_inc(pe_bias, 1)
            router_first(0, None)
            router_second(0, None)
            run(pe, step, -2, STEPS + 1)


def build(nc):
    x = nc.dram_tensor("x", (B, C, H, W), F32, kind="ExternalInput").ap()
    experts = nc.dram_tensor("experts", (E, P, X_LEN), F32, kind="ExternalInput").ap()
    shared = nc.dram_tensor("shared", (P, S_LEN), F32, kind="ExternalInput").ap()
    zeros = nc.dram_tensor("zeros", (32, GROUPS, W), F32, kind="ExternalInput").ap()
    out = nc.dram_tensor("out", (B, C, H, W), F32, kind="ExternalOutput").ap()
    moe_conv_kernel(nc, x, experts, shared, zeros, out)


def pack_experts(a):
    packed = np.zeros((E, P, X_LEN), np.float32)
    packed[:, :, X_EXP:X_EXP + 256] = a["L0_conv_ew_exp"].transpose(0, 2, 1)
    proj = a["L0_conv_ew_proj"].transpose(0, 2, 1).reshape(E, 2, P, P)
    packed[:, :, X_PROJ:X_PROJ + 256] = proj.transpose(0, 2, 1, 3).reshape(E, P, 256)
    dw = a["L0_conv_ew_dw"].reshape(E, 2, P, 9)
    packed[:, :, X_DW:X_DW + 18] = dw.transpose(0, 2, 1, 3).reshape(E, P, 18)
    for col, name in ((X_S1, "e1s"), (X_B1, "e1b"), (X_S2, "e2s"), (X_B2, "e2b")):
        packed[:, :, col:col + 2] = a["L0_conv_" + name].reshape(E, 2, P).transpose(0, 2, 1)
    packed[:, :, X_S3:X_S3 + P] = a["L0_conv_e3s"][:, None, :]
    return packed


def pack_shared(a):
    packed = np.zeros((P, S_LEN), np.float32)
    packed[:, S_SPW:S_SPW + P] = a["L0_conv_sw_pw"].T
    packed[:, S_PW:S_PW + 512] = a["L0_conv_pw"].T.reshape(2, P, C).transpose(1, 0, 2).reshape(P, 512)
    packed[:, S_BNS:S_BNS + C] = a["L0_conv_bn_s"][None, :]
    packed[:, S_BNB:S_BNB + 2] = a["L0_conv_bn_b"].reshape(2, P).T
    for n, name in enumerate(("sbn1_s", "sbn1_b", "sbn2_s", "sbn2_b")):
        packed[:, S_SBN + n] = a["L0_conv_" + name]
    packed[:, S_RW1:S_RW1 + R] = a["L0_conv_rw1"].T
    packed[0:R, S_RW2:S_RW2 + E] = a["L0_conv_rw2"].T
    packed[0:R, S_RB1] = a["L0_conv_rb1"]
    packed[:, S_RB2:S_RB2 + E] = a["L0_conv_rb2"][None, :]
    packed[:, S_B3:S_B3 + E] = a["L0_conv_e3b"].T
    dw = a["L0_conv_sw_dw"].reshape(GROUPS, 32, 3, 3).transpose(2, 1, 0, 3)
    packed[0:32 * SLOTS, S_CONV:S_EYE] = dw.reshape(32 * SLOTS, GROUPS * 3)
    packed[:, S_EYE:S_EYE + 32] = np.tile(np.eye(32, dtype=np.float32), (4, 1))
    packed[:, S_TRI:S_TRI + E * E] = np.tril(np.ones((E, E), np.float32), -1).reshape(1, E * E)
    packed[:, S_IOTA:S_IOTA + E] = np.arange(E, dtype=np.float32)[None, :]
    return packed


def kernel(**inputs):
    import concourse.bacc as bacc
    from concourse.bass_utils import run_bass_kernel_spmd

    a = {n: np.asarray(v) for n, v in inputs.items()}
    arrays = {
        "x": np.ascontiguousarray(a["x"]),
        "experts": pack_experts(a),
        "shared": pack_shared(a),
        "zeros": np.zeros((32, GROUPS, W), np.float32),
    }
    nc = bacc.Bacc("TRN2", target_bir_lowering=False, num_devices=1)
    build(nc)
    r = run_bass_kernel_spmd(nc, [arrays], core_ids=[0])
    return r.results[0]["out"]
```

```python
from contextlib import ExitStack

import numpy as np

import concourse.bass as bass
from concourse import mybir

F32 = mybir.dt.float32
BF16 = mybir.dt.bfloat16
I32 = mybir.dt.int32
ALU = mybir.AluOpType
ACT = mybir.ActivationFunctionType
AX_X = mybir.AxisListType.X

P = 128
B, C, H, W = 16, 256, 64, 64
E, K, R = 4, 2, 16
CHUNKS = 4
ROWS = H // CHUNKS
PX = ROWS * W
HALF = PX // 2
BLOCKS = 4
STEPS = B * CHUNKS
PAIR = 2 * CHUNKS
SLOTS = 3
GROUPS = P // 32

X_EXP = 0
X_PROJ = X_EXP + 256
X_DW = X_PROJ + 256
X_S1, X_B1 = X_DW + 18, X_DW + 20
X_S2, X_B2 = X_DW + 22, X_DW + 24
X_S3 = X_DW + 26
X_LEN = X_S3 + 128

S_SPW = 0
S_PW = S_SPW + 128
S_BNS = S_PW + 512
S_BNB = S_BNS + 256
S_SBN = S_BNB + 2
S_RW1 = S_SBN + 4
S_RW2 = S_RW1 + R
S_RB1 = S_RW2 + E
S_RB2 = S_RB1 + 1
S_B3 = S_RB2 + E
S_CONV = S_B3 + E
S_EYE = S_CONV + GROUPS * 3
S_TRI = S_EYE + 32
S_IOTA = S_TRI + E * E
S_LEN = S_IOTA + E

POOL_TAPS = [(0, 0), (0, -1), (0, 1), (-1, -1)]
FULL_BELOW = [(1, 0), (-1, 0), (-1, 1), (1, -1), (1, 1)]
FULL_ABOVE = [(-1, 0), (1, 0), (-1, 1), (1, -1), (1, 1)]
NP, NV = len(POOL_TAPS), len(FULL_BELOW)


def vector_taps(c):
    return FULL_ABOVE if c == CHUNKS - 1 else FULL_BELOW


def tap_index(dy, dx):
    return 3 * (dy + 1) + dx + 1


def region(c, dy, dx):
    r0, r1 = max(ROWS * c, -dy), min(ROWS * (c + 1), H - dy)
    x0, x1 = max(0, -dx), W - max(0, dx)
    return r0, r1, x0, x1


def router_step(k):
    return k % CHUNKS == 1 and 0 < k < STEPS - CHUNKS


def plan_psum():
    order = [("bias", 0, 0), ("gate1", -1, 0), ("gate2", -1, 0)]
    for k in range(-2, STEPS + 1):
        order += groups_of(k)
    return {g: (n % 2, order[n - 2] if n >= 2 else None) for n, g in enumerate(order)}


def groups_of(k):
    prev, cur, nxt = 1 <= k, 0 <= k < STEPS, k + 2 < STEPS
    out = []
    if prev:
        out.append(("proj", k - 1, 0))
    if nxt:
        out.append(("expand", k + 2, 0))
    if prev:
        out.append(("final", k - 1, 0))
    if nxt:
        out.append(("expand", k + 2, 1))
    if router_step(k):
        out.append(("gate1", k // CHUNKS, 0))
    if nxt:
        out.append(("expand", k + 2, 2))
    if router_step(k):
        out.append(("gate2", k // CHUNKS, 0))
    if cur:
        out.append(("sconv", k, 0))
    if nxt:
        out.append(("expand", k + 2, 3))
    if prev:
        out.append(("final", k - 1, 1))
    if cur:
        out.append(("spw", k, 0))
    return out


def moe_conv_kernel(nc, x, experts, shared, zeros, out):
    with ExitStack() as ctx:
        def sb(name, shape, dt=F32):
            return ctx.enter_context(nc.sbuf_tensor(name, [P, *shape], dt))

        def sem(name):
            return ctx.enter_context(nc.semaphore(name))

        x_d = sb("x_d", [2, H, W])
        x_res = sb("x_res", [2, ROWS, W])
        x_slot = sb("x_slot", [GROUPS, ROWS, W])
        h = sb("h", [BLOCKS, H, W])
        part_sum = sb("part_sum", [BLOCKS, ROWS, W])
        prod = sb("prod", [NP - 1, ROWS, W])
        h2 = sb("h2", [BLOCKS, PX])
        h2s = sb("h2s", [PX])
        out_s = sb("out_s", [PX])
        out_d = sb("out_d", [PX])
        sel = sb("sel", [2, K, X_LEN])
        proj_w = sb("proj_w", [2, K, 256])
        stat = sb("stat", [S_LEN])
        conv_w = sb("conv_w", [GROUPS * 3, 32])
        pw_s = sb("pw_s", [2, 256])
        b3_out = sb("b3_out", [2, E])
        junk = sb("junk", [PX], BF16)
        xsum = sb("xsum", [CHUNKS])
        gate_h = sb("gate_h", [P])
        logit = sb("logit", [E])
        lmax = sb("lmax", [1])
        zed = sb("zed", [E])
        zsilu = sb("zsilu", [E])
        above = sb("above", [E, E])
        equal = sb("equal", [E, E])
        rank = sb("rank", [E])
        tmp = sb("tmp", [E])
        idx_f = sb("idx_f", [K])
        idx = sb("idx", [K], I32)
        den = sb("den", [E])
        prob = sb("prob", [E])
        psumz = sb("psumz", [1])
        gate = sb("gate", [2, K])
        gate_all = sb("gate_all", [E])
        gate_sum = sb("gate_sum", [2, 1])
        fb_terms = sb("fb_terms", [2, E])
        fb_sum = sb("fb_sum", [2])
        fbias = sb("fbias", [2, 2])

        acc = [ctx.enter_context(nc.psum_tensor(f"acc{s}", [P, ROWS, W], F32)) for s in range(2)]
        mm = [ctx.enter_context(nc.psum_tensor(f"mm{s}", [P, PX], F32)) for s in range(2)]

        rate = {}

        def counter(name, per_pair):
            s = sem(name)
            rate[s.name] = per_pair
            return s

        stat_in = sem("stat_in")
        sp_passed = sem("sp_passed")
        setup = sem("setup")
        pe_bias = sem("pe_bias")
        xd_in = [[counter(f"xd_in{p}{c}", 16) for c in range(CHUNKS)] for p in range(2)]
        xres_in = [counter(f"xres_in{s}", 16 * PAIR // 2) for s in range(2)]
        xslot_in = counter("xslot_in", 16 * 14 * 2)
        sel_in = [counter(f"sel_in{p}", 16 * K) for p in range(2)]
        st_d = [[counter(f"st_d{p}{c}", 16) for c in range(CHUNKS)] for p in range(2)]
        st_s = [counter(f"st_s{s}", 16 * PAIR // 2) for s in range(2)]
        pe_expand = counter("pe_expand", BLOCKS * PAIR)
        pe_sconv = counter("pe_sconv", PAIR)
        pe_spw = counter("pe_spw", PAIR)
        pe_proj = counter("pe_proj", PAIR)
        pe_final = counter("pe_final", 2 * PAIR)
        pe_gate1 = counter("pe_gate1", 2)
        pe_gate2 = counter("pe_gate2", 2)
        act_h = counter("act_h", BLOCKS * PAIR)
        act_prod = counter("act_prod", NP * BLOCKS * PAIR)
        act_h2 = counter("act_h2", BLOCKS * PAIR)
        act_h2s = counter("act_h2s", PAIR)
        act_outs = counter("act_outs", PAIR)
        act_sum = counter("act_sum", CHUNKS * 2)
        act_gate = counter("act_gate", 2)
        act_zsilu = counter("act_zsilu", 2)
        pool_add = counter("pool_add", (NP - 1) * BLOCKS * PAIR)
        dve_tap = [counter(f"dve_tap{s}", NV * BLOCKS // 2 * PAIR) for s in range(2)]
        dve_outd = counter("dve_outd", PAIR)
        dve_out = counter("dve_out", 2 * PAIR)
        N_CHOOSE, N_GATE = 11, 13
        dve_choose = counter("dve_choose", 2 * N_CHOOSE)
        dve_gate = counter("dve_gate", 2 * N_GATE)

        def due(s, value, lap):
            return value if lap is None else lap * rate[s.name] + value

        def image(k, lap):
            i = k // CHUNKS
            return i if lap is None else i + 2 * lap

        def run(eng, step, first, last):
            for k in range(first, PAIR):
                step(k, None)
            with eng.Fori(0, STEPS // PAIR - 2) as lap:
                for k in range(PAIR, 2 * PAIR):
                    step(k, lap)
            for k in range(STEPS - PAIR, last):
                step(k, None)

        def expands(k, b): return BLOCKS * k + b + 1
        def prods(k, b, n): return NP * (BLOCKS * k + b) + n + 1
        def adds(k, b, n): return (NP - 1) * (BLOCKS * k + b) + n + 1
        def h2s_of(k, b): return BLOCKS * k + b + 1
        def taps(k, b, t): return NV * (2 * k + b // 2) + t + 1
        def finals(k, m): return 2 * k + m + 1
        def xd_loads(k): return 16 * (k // PAIR + 1)
        def xres_loads(k): return 16 * (k // 2 + 1)
        def xslot_loads(k): return 16 * (14 * (k // CHUNKS) + (4, 7, 10, 14)[k % CHUNKS])

        plan = plan_psum()
        drain = {
            "bias": lambda k, n: (setup, 3),
            "gate1": lambda k, n: (act_gate, k + 2),
            "gate2": lambda k, n: (dve_choose, N_CHOOSE * (k + 1) + 1),
            "proj": lambda k, n: (dve_outd, k + 1),
            "final": lambda k, n: (dve_out, finals(k, n)),
            "expand": lambda k, n: (act_h, expands(k, n)),
            "sconv": lambda k, n: (act_h2s, k + 1),
            "spw": lambda k, n: (act_outs, k + 1),
        }

        def weights(par, slot, col, n=1):
            return sel[:, par, slot, col:col + n]

        block = ctx.enter_context(nc.Block())

        @block.sync
        def _(sp):
            def load_xd(i_static, c, i):
                sp.dma_start(x_d[:, i_static % 2, ROWS * c:ROWS * (c + 1), :],
                             x[i, P:, ROWS * c:ROWS * (c + 1), :]).then_inc(xd_in[i_static % 2][c], 16)

            def load_res(k, lap):
                c = k % CHUNKS
                sp.dma_start(x_res[:, k % 2], x[image(k, lap), 0:P, ROWS * c:ROWS * (c + 1), :]
                             ).then_inc(xres_in[k % 2], 16)

            def load_slots(k, lap):
                c, i = k % CHUNKS, image(k, lap)
                src = x[i, 0:P].rearrange("(g c) y w -> c g y w", g=GROUPS)
                for j in range(SLOTS):
                    r0, r1, _, _ = region(c, j - 1, 0)
                    part = x_slot[32 * j:32 * (j + 1)]
                    sp.dma_start(part[:, :, r0 - ROWS * c:r1 - ROWS * c, :], src[:, :, r0 + j - 1:r1 + j - 1, :]
                                 ).then_inc(xslot_in, 16)
                    if r1 - r0 < ROWS:
                        edge = 0 if j == 0 else ROWS - 1
                        sp.dma_start(part[:, :, edge, :], zeros).then_inc(xslot_in, 16)

            def fetch_experts(i_static, lap):
                par = i_static % 2
                sp.wait_ge(dve_choose, due(dve_choose, N_CHOOSE * (i_static + 1), lap))
                sp.sem_inc(sp_passed, 1)
                if i_static >= 2:
                    sp.wait_ge(pe_proj, due(pe_proj, CHUNKS * (i_static - 1), lap))
                    sp.sem_inc(sp_passed, 1)
                for s in range(K):
                    e = sp.value_load(idx[0:1, s:s + 1], min_val=0, max_val=E - 1)
                    sp.dma_start(sel[:, par, s, :], experts[bass.ds(e, 1), :, :].rearrange("a p l -> (a p) l")
                                 ).then_inc(sel_in[par], 16)

            def step(k, lap):
                if k % CHUNKS == 2 and router_step(k - 1):
                    fetch_experts(k // CHUNKS + 1, lap)
                c, kp = (k - 1) % CHUNKS, k - 1
                if k >= 1:
                    sp.wait_ge(dve_out, due(dve_out, finals(kp, 0), lap))
                    sp.sem_inc(sp_passed, 1)
                    sp.dma_start(out[image(kp, lap), 0:P, ROWS * c:ROWS * (c + 1), :], x_res[:, kp % 2]
                                 ).then_inc(st_s[kp % 2], 16)
                if k + 1 < STEPS:
                    sp.wait_ge(pe_sconv, due(pe_sconv, k + 1, lap))
                    sp.sem_inc(sp_passed, 1)
                    load_slots(k + 1, lap)
                if k >= 1:
                    par = (kp // CHUNKS) % 2
                    sp.wait_ge(dve_out, due(dve_out, finals(kp, 1), lap))
                    sp.sem_inc(sp_passed, 1)
                    sp.dma_start(out[image(kp, lap), P:, ROWS * c:ROWS * (c + 1), :],
                                 x_d[:, par, ROWS * c:ROWS * (c + 1), :]).then_inc(st_d[par][c], 16)
                    if k + 1 < STEPS:
                        sp.wait_ge(st_s[kp % 2], due(st_s[kp % 2], xres_loads(kp), lap))
                        sp.sem_inc(sp_passed, 1)
                        load_res(k + 1, lap)
                    if kp // CHUNKS + 2 < B:
                        sp.wait_ge(st_d[par][c], due(st_d[par][c], xd_loads(kp), lap))
                        sp.sem_inc(sp_passed, 1)
                        load_xd(kp // CHUNKS + 2, c, image(kp, lap) + 2)

            sp.dma_start(stat[:], shared).then_inc(stat_in, 16)
            for c in range(CHUNKS):
                load_xd(0, c, 0)
            fetch_experts(0, None)
            load_slots(0, None)
            load_res(0, None)
            load_res(1, None)
            for c in range(CHUNKS):
                load_xd(1, c, 1)
            run(sp, step, 0, STEPS + 1)
            for s in range(2):
                sp.wait_ge(st_s[s], 16 * STEPS // 2)
                for c in range(CHUNKS):
                    sp.wait_ge(st_d[s][c], 16 * B // 2)

        @block.gpsimd
        def _(pool):
            def step(k, lap):
                c = k % CHUNKS
                for b in range(BLOCKS):
                    for n in range(1, NP):
                        r0, r1, x0, x1 = region(c, *POOL_TAPS[n])
                        total = part_sum[:, b, r0 - ROWS * c:r1 - ROWS * c, x0:x1]
                        pool.wait_ge(act_prod, due(act_prod, prods(k, b, n), lap))
                        if n > 1:
                            pool.wait_ge(pool_add, due(pool_add, adds(k, b, n - 2), lap))
                        nc.gpsimd.tensor_tensor(total, total, prod[:, n - 1, r0 - ROWS * c:r1 - ROWS * c, x0:x1],
                                                ALU.add).then_inc(pool_add, 1)
            run(pool, step, 0, STEPS)

        @block.scalar
        def _(act):
            def sum_x(k, lap):
                c, par = k % CHUNKS, (k // CHUNKS) % 2
                act.wait_ge(xd_in[par][c], due(xd_in[par][c], xd_loads(k), lap))
                if k >= CHUNKS:
                    act.wait_ge(pe_gate1, due(pe_gate1, k // CHUNKS, lap))
                if k >= 1:
                    act.wait_ge(act_sum, due(act_sum, k, lap))
                nc.scalar.activation(junk[:], x_d[:, par, ROWS * c:ROWS * (c + 1), :].rearrange("p y w -> p (y w)"),
                                     ACT.Copy, accum_out=xsum[:, c:c + 1]).then_inc(act_sum, 1)

            def router_hidden(i_static, lap):
                buf = plan[("gate1", i_static - 1, 0)][0]
                act.wait_ge(pe_gate1, due(pe_gate1, i_static + 1, lap))
                if i_static >= 1:
                    act.wait_ge(pe_gate2, due(pe_gate2, i_static, lap))
                nc.scalar.activation(gate_h[0:R, :], mm[buf][0:R, 0:P], ACT.Silu, bias=stat[0:R, S_RB1:S_RB1 + 1],
                                     scale=1.0 / (H * W)).then_inc(act_gate, 1)

            def router_silu(i_static, lap):
                act.wait_ge(dve_choose, due(dve_choose, N_CHOOSE * i_static + 3, lap))
                nc.scalar.activation(zsilu[:], zed[:], ACT.Silu).then_inc(act_zsilu, 1)

            def expand_out(k, b, lap):
                c, par = k % CHUNKS, (k // CHUNKS) % 2
                act.wait_ge(pe_expand, due(pe_expand, expands(k, b), lap))
                if k >= 3:
                    act.wait_ge(dve_tap[b % 2], due(dve_tap[b % 2], taps(k - 3, b, NV - 1), lap))
                nc.scalar.activation(h[:, b, ROWS * c:ROWS * (c + 1), :].rearrange("p y w -> p (y w)"),
                                     mm[plan[("expand", k, b)][0]][:], ACT.Silu,
                                     bias=weights(par, b // 2, X_B1 + b % 2), scale=weights(par, b // 2, X_S1 + b % 2)
                                     ).then_inc(act_h, 1)

            def product(k, b, n, lap):
                c, par = k % CHUNKS, (k // CHUNKS) % 2
                dy, dx = POOL_TAPS[n]
                r0, r1, x0, x1 = region(c, dy, dx)
                if n == 0:
                    act.wait_ge(act_h, due(act_h, expands(k, b), lap))
                    if k >= 1:
                        act.wait_ge(dve_tap[b % 2], due(dve_tap[b % 2], taps(k - 1, b, 0), lap))
                    dst = part_sum[:, b]
                else:
                    if k >= 1 or b >= 1:
                        act.wait_ge(pool_add, due(pool_add, adds(k, b, n - 1) - (NP - 1), lap))
                    dst = prod[:, n - 1]
                nc.scalar.activation(dst[:, r0 - ROWS * c:r1 - ROWS * c, x0:x1], h[:, b, r0 + dy:r1 + dy, x0 + dx:x1 + dx],
                                     ACT.Copy, scale=weights(par, b // 2, X_DW + 9 * (b % 2) + tap_index(dy, dx))
                                     ).then_inc(act_prod, 1)

            def expert_out(k, b, lap):
                par = (k // CHUNKS) % 2
                act.wait_ge(dve_tap[b % 2], due(dve_tap[b % 2], taps(k, b, NV - 1), lap))
                if k >= 1:
                    act.wait_ge(pe_proj, due(pe_proj, k, lap))
                nc.scalar.activation(h2[:, b, :], acc[b % 2][:].rearrange("p y w -> p (y w)"), ACT.Silu,
                                     bias=weights(par, b // 2, X_B2 + b % 2), scale=weights(par, b // 2, X_S2 + b % 2)
                                     ).then_inc(act_h2, 1)

            def shared_hidden(k, lap):
                act.wait_ge(pe_sconv, due(pe_sconv, k + 1, lap))
                if k >= 1:
                    act.wait_ge(pe_spw, due(pe_spw, k, lap))
                nc.scalar.activation(h2s[:], mm[plan[("sconv", k, 0)][0]][:], ACT.Silu, bias=stat[:, S_SBN + 1:S_SBN + 2], scale=stat[:, S_SBN:S_SBN + 1]
                                     ).then_inc(act_h2s, 1)

            def shared_out(k, lap):
                act.wait_ge(pe_spw, due(pe_spw, k + 1, lap))
                if k >= 1:
                    act.wait_ge(pe_final, due(pe_final, finals(k - 1, 1), lap))
                nc.scalar.activation(out_s[:], mm[plan[("spw", k, 0)][0]][:], ACT.Silu,
                                     bias=stat[:, S_SBN + 3:S_SBN + 4], scale=stat[:, S_SBN + 2:S_SBN + 3]
                                     ).then_inc(act_outs, 1)

            def step(k, lap):
                prev, cur, nxt = 1 <= k, 0 <= k < STEPS, k + 2 < STEPS
                ahead = 0 <= k + 1 < STEPS
                if k % CHUNKS == 2 and router_step(k - 1):
                    router_silu(k // CHUNKS + 1, lap)
                if cur:
                    product(k, 2, 0, lap)
                if prev:
                    shared_out(k - 1, lap)
                if cur:
                    product(k, 2, 1, lap)
                    product(k, 2, 2, lap)
                if prev:
                    expert_out(k - 1, 3, lap)
                if cur:
                    product(k, 2, 3, lap)
                    product(k, 3, 0, lap)
                    product(k, 3, 1, lap)
                if nxt:
                    expand_out(k + 2, 0, lap)
                if cur:
                    product(k, 3, 2, lap)
                    expert_out(k, 0, lap)
                    product(k, 3, 3, lap)
                if CHUNKS <= k + 6 < STEPS:
                    sum_x(k + 6, lap)
                if ahead:
                    product(k + 1, 0, 0, lap)
                if nxt:
                    expand_out(k + 2, 1, lap)
                if router_step(k):
                    router_hidden(k // CHUNKS + 1, lap)
                if ahead:
                    product(k + 1, 0, 1, lap)
                if nxt:
                    expand_out(k + 2, 2, lap)
                if cur:
                    expert_out(k, 1, lap)
                if ahead:
                    product(k + 1, 0, 2, lap)
                    product(k + 1, 0, 3, lap)
                    product(k + 1, 1, 0, lap)
                if cur:
                    shared_hidden(k, lap)
                if ahead:
                    product(k + 1, 1, 1, lap)
                if cur:
                    expert_out(k, 2, lap)
                if nxt:
                    expand_out(k + 2, 3, lap)
                if ahead:
                    product(k + 1, 1, 2, lap)
                    product(k + 1, 1, 3, lap)

            for k in range(CHUNKS):
                sum_x(k, None)
            act.wait_ge(stat_in, 16)
            router_hidden(0, None)
            router_silu(0, None)
            act.wait_ge(sel_in[0], 16 * K)
            run(act, step, -2, STEPS + 1)

        @block.vector
        def _(dve):
            def choose(i_static, part, lap):
                done = N_CHOOSE * i_static
                by_f = logit[:].unsqueeze(1).broadcast_to([P, E, E])
                by_e = logit[:].unsqueeze(2).broadcast_to([P, E, E])
                if part == 0:
                    buf = plan[("gate2", i_static - 1, 0)][0]
                    dve.wait_ge(pe_gate2, due(pe_gate2, i_static + 1, lap))
                    if i_static >= 1:
                        dve.wait_ge(act_zsilu, due(act_zsilu, i_static, lap))
                    nc.vector.tensor_tensor(logit[:], mm[buf][:, 0:E], stat[:, S_RB2:S_RB2 + E], ALU.add).then_inc(dve_choose, 1)
                    dve.wait_ge(dve_choose, due(dve_choose, done + 1, lap))
                    nc.vector.reduce_max(lmax[:], logit[:], AX_X).then_inc(dve_choose, 1)
                elif part == 1:
                    dve.wait_ge(dve_choose, due(dve_choose, done + 2, lap))
                    nc.vector.tensor_scalar(zed[:], logit[:], lmax[:], -1.0, ALU.subtract, ALU.add).then_inc(dve_choose, 1)
                    nc.vector.tensor_tensor(equal[:], by_f, by_e, ALU.is_equal).then_inc(dve_choose, 1)
                    nc.vector.tensor_tensor(above[:], by_f, by_e, ALU.is_gt).then_inc(dve_choose, 1)
                elif part == 2:
                    dve.wait_ge(dve_choose, due(dve_choose, done + 5, lap))
                    nc.vector.tensor_tensor(equal[:], equal[:], stat[:, S_TRI:S_TRI + E * E].rearrange("p (e f) -> p e f", e=E),
                                            ALU.mult).then_inc(dve_choose, 1)
                    dve.wait_ge(dve_choose, due(dve_choose, done + 6, lap))
                    nc.vector.tensor_tensor(above[:], above[:], equal[:], ALU.add).then_inc(dve_choose, 1)
                elif part == 3:
                    dve.wait_ge(dve_choose, due(dve_choose, done + 7, lap))
                    if i_static >= 1:
                        dve.wait_ge(dve_gate, due(dve_gate, N_GATE * i_static, lap))
                    nc.vector.reduce_sum(rank[:], above[:], AX_X).then_inc(dve_choose, 1)
                    dve.wait_ge(dve_choose, due(dve_choose, done + 8, lap))
                    nc.vector.scalar_tensor_tensor(tmp[:], rank[:], 0.0, stat[:, S_IOTA:S_IOTA + E], ALU.is_equal,
                                                   ALU.mult, accum_out=idx_f[:, 0:1]).then_inc(dve_choose, 1)
                else:
                    dve.wait_ge(dve_choose, due(dve_choose, done + 9, lap))
                    nc.vector.scalar_tensor_tensor(tmp[:], rank[:], 1.0, stat[:, S_IOTA:S_IOTA + E], ALU.is_equal,
                                                   ALU.mult, accum_out=idx_f[:, 1:2]).then_inc(dve_choose, 1)
                    dve.wait_ge(dve_choose, due(dve_choose, done + 10, lap))
                    nc.vector.tensor_copy(idx[:], idx_f[:]).then_inc(dve_choose, 1)

            def gates(i_static, part, lap):
                done, par = N_GATE * i_static, i_static % 2
                if part == 0:
                    dve.wait_ge(act_zsilu, due(act_zsilu, i_static + 1, lap))
                    nc.vector.tensor_tensor(den[:], zed[:], zsilu[:], ALU.subtract).then_inc(dve_gate, 1)
                elif part == 1:
                    dve.wait_ge(dve_gate, due(dve_gate, done + 1, lap))
                    nc.vector.reciprocal(den[:], den[:]).then_inc(dve_gate, 1)
                elif part == 2:
                    dve.wait_ge(dve_gate, due(dve_gate, done + 2, lap))
                    nc.vector.scalar_tensor_tensor(prob[:], zsilu[:], 1.0, den[:], ALU.mult, ALU.mult,
                                                   accum_out=psumz[:]).then_inc(dve_gate, 1)
                elif part == 3:
                    dve.wait_ge(dve_gate, due(dve_gate, done + 3, lap))
                    nc.vector.reciprocal(psumz[:], psumz[:]).then_inc(dve_gate, 1)
                elif part == 4:
                    dve.wait_ge(dve_gate, due(dve_gate, done + 4, lap))
                    nc.vector.tensor_scalar(prob[:], prob[:], psumz[:], None, ALU.mult).then_inc(dve_gate, 1)
                elif part in (5, 6):
                    s = part - 5
                    dve.wait_ge(dve_gate, due(dve_gate, done + 5 + s, lap))
                    nc.vector.scalar_tensor_tensor(tmp[:], rank[:], float(s), prob[:], ALU.is_equal, ALU.mult,
                                                   accum_out=gate[:, par, s:s + 1]).then_inc(dve_gate, 1)
                elif part == 7:
                    nc.vector.scalar_tensor_tensor(gate_all[:], rank[:], float(K), prob[:], ALU.is_lt, ALU.mult,
                                                   accum_out=gate_sum[:, par, :]).then_inc(dve_gate, 1)
                elif part == 8:
                    dve.wait_ge(dve_gate, due(dve_gate, done + 8, lap))
                    nc.vector.tensor_tensor(fb_terms[:], b3_out[:], gate_all[:].unsqueeze(1).broadcast_to([P, 2, E]),
                                            ALU.mult).then_inc(dve_gate, 1)
                elif part == 9:
                    dve.wait_ge(dve_gate, due(dve_gate, done + 9, lap))
                    nc.vector.reduce_sum(fb_sum[:], fb_terms[:], AX_X).then_inc(dve_gate, 1)
                elif part == 10:
                    dve.wait_ge(dve_gate, due(dve_gate, done + 10, lap))
                    nc.vector.tensor_tensor(fbias[:, par, :], fb_sum[:], stat[:, S_BNB:S_BNB + 2], ALU.add).then_inc(dve_gate, 1)
                else:
                    s = part - 11
                    dve.wait_ge(sel_in[par], due(sel_in[par], 16 * K * (i_static // 2 + 1), lap))
                    if i_static >= 2:
                        dve.wait_ge(pe_proj, due(pe_proj, CHUNKS * (i_static - 1), lap))
                    nc.vector.scalar_tensor_tensor(
                        proj_w[:, par, s, :].rearrange("p (b o) -> p b o", b=2),
                        weights(par, s, X_PROJ, 256).rearrange("p (b o) -> p b o", b=2), gate[:, par, s:s + 1],
                        weights(par, s, X_S3, P).unsqueeze(1).broadcast_to([P, 2, P]),
                        ALU.mult, ALU.mult).then_inc(dve_gate, 1)

            def tap(k, b, t, lap):
                c, par = k % CHUNKS, (k // CHUNKS) % 2
                dy, dx = vector_taps(c)[t]
                r0, r1, x0, x1 = region(c, dy, dx)
                dst = acc[b % 2][:, r0 - ROWS * c:r1 - ROWS * c, x0:x1]
                if t == 0:
                    dve.wait_ge(pool_add, due(pool_add, adds(k, b, NP - 2), lap))
                    if c < CHUNKS - 1:
                        dve.wait_ge(act_h, due(act_h, expands(k + 1, b), lap))
                    if k >= 1 or b >= 2:
                        dve.wait_ge(act_h2, due(act_h2, h2s_of(k, b) - 2, lap))
                    before = part_sum[:, b]
                else:
                    dve.wait_ge(dve_tap[b % 2], due(dve_tap[b % 2], taps(k, b, t - 1), lap))
                    before = dst
                nc.vector.scalar_tensor_tensor(dst, h[:, b, r0 + dy:r1 + dy, x0 + dx:x1 + dx],
                                               weights(par, b // 2, X_DW + 9 * (b % 2) + tap_index(dy, dx)), before,
                                               ALU.mult, ALU.add).then_inc(dve_tap[b % 2], 1)

            def expert_sum(k, lap):
                c, par = k % CHUNKS, (k // CHUNKS) % 2
                dve.wait_ge(pe_proj, due(pe_proj, k + 1, lap))
                if k >= 1:
                    dve.wait_ge(pe_final, due(pe_final, finals(k - 1, 1), lap))
                dve.wait_ge(xd_in[par][c], due(xd_in[par][c], xd_loads(k), lap))
                nc.vector.scalar_tensor_tensor(out_d[:], x_d[:, par, ROWS * c:ROWS * (c + 1), :].rearrange("p y w -> p (y w)"),
                                               gate_sum[:, par, :], mm[plan[("proj", k, 0)][0]][:],
                                               ALU.mult, ALU.add).then_inc(dve_outd, 1)

            def output(k, m, lap):
                c, par = k % CHUNKS, (k // CHUNKS) % 2
                dve.wait_ge(pe_final, due(pe_final, finals(k, m), lap))
                if m == 0:
                    dve.wait_ge(xres_in[k % 2], due(xres_in[k % 2], xres_loads(k), lap))
                    place = x_res[:, k % 2].rearrange("p y w -> p (y w)")
                else:
                    dve.wait_ge(dve_outd, due(dve_outd, k + 1, lap))
                    place = x_d[:, par, ROWS * c:ROWS * (c + 1), :].rearrange("p y w -> p (y w)")
                nc.vector.scalar_tensor_tensor(place, mm[plan[("final", k, m)][0]][:], fbias[:, par, m:m + 1], place,
                                               ALU.add, ALU.add).then_inc(dve_out, 1)

            def between(k, place, lap):
                prev = 1 <= k
                if prev and place == 6:
                    expert_sum(k - 1, lap)
                if prev and place == 9:
                    output(k - 1, 0, lap)
                if prev and place == 19:
                    output(k - 1, 1, lap)
                if router_step(k) and place >= 15:
                    choose(k // CHUNKS + 1, place - 15, lap)
                if k % CHUNKS == 2 and router_step(k - 1) and 7 <= place:
                    gates(k // CHUNKS + 1, place - 7, lap)

            def step(k, lap):
                for b in range(BLOCKS):
                    kb, bb = (k, b - 1) if b else (k - 1, BLOCKS - 1)
                    if b % 2 == 0:
                        slot = ((k, b, 0), (kb, bb, 3), (k, b, 1), (kb, bb, 4), (k, b, 2))
                    else:
                        slot = ((kb, bb, 3), (k, b, 0), (kb, bb, 4), (k, b, 1), (k, b, 2))
                    for n, (kt, bt, t) in enumerate(slot):
                        if 0 <= kt < STEPS:
                            tap(kt, bt, t, lap)
                        between(k, NV * b + n, lap)

            dve.wait_ge(stat_in, 16)
            nc.vector.tensor_tensor(pw_s[:], stat[:, S_PW:S_PW + 512].rearrange("p (k o) -> p k o", k=2),
                                    stat[:, S_BNS:S_BNS + 256].unsqueeze(1).broadcast_to([P, 2, 256]),
                                    ALU.mult).then_inc(setup, 1)
            nc.vector.tensor_tensor(conv_w[:], stat[:, S_CONV:S_EYE].unsqueeze(2).broadcast_to([P, GROUPS * 3, 32]),
                                    stat[:, S_EYE:S_EYE + 32].unsqueeze(1).broadcast_to([P, GROUPS * 3, 32]),
                                    ALU.mult).then_inc(setup, 1)
            dve.wait_ge(pe_bias, 1)
            nc.vector.tensor_copy(b3_out[:], mm[plan[("bias", 0, 0)][0]][:, 0:2 * E].rearrange("p (m e) -> p m e", m=2)
                                  ).then_inc(setup, 1)
            dve.wait_ge(setup, 3)
            for part in range(5):
                choose(0, part, None)
            for part in range(13):
                gates(0, part, None)
            dve.wait_ge(dve_gate, N_GATE)
            run(dve, step, 0, STEPS + 1)

        @block.tensor
        def _(pe):
            def drained(group, lap):
                name, k, n = plan[group][1]
                s, value = drain[name](k, n)
                return s, due(s, value, lap)

            def expand(k, b, lap):
                c, par = k % CHUNKS, (k // CHUNKS) % 2
                ps = mm[plan[("expand", k, b)][0]]
                pe.wait_ge(*drained(("expand", k, b), lap))
                pe.wait_ge(xd_in[par][c], due(xd_in[par][c], xd_loads(k), lap))
                pe.wait_ge(sel_in[par], due(sel_in[par], 16 * K * (k // PAIR + 1), lap))
                for n in range(2):
                    mmul = nc.tensor.matmul(ps[:, HALF * n:HALF * (n + 1)],
                                            weights(par, b // 2, X_EXP + P * (b % 2), P),
                                            x_d[:, par, ROWS * c + ROWS // 2 * n:ROWS * c + ROWS // 2 * (n + 1), :],
                                            start=True, stop=True)
                mmul.then_inc(pe_expand, 1)

            def shared_conv(k, lap):
                ps = mm[plan[("sconv", k, 0)][0]]
                pe.wait_ge(*drained(("sconv", k, 0), lap))
                pe.wait_ge(xslot_in, due(xslot_in, xslot_loads(k), lap))
                rows = ROWS // 2
                for n in range(2):
                    for t, dx in enumerate((0, -1, 1)):
                        x0, x1 = max(0, -dx), W - max(0, dx)
                        for g in range(GROUPS):
                            dst = ps[32 * g:32 * (g + 1), HALF * n:HALF * (n + 1)].rearrange("p (y w) -> p y w", w=W)
                            mmul = nc.tensor.matmul(dst[:, :, x0:x1], conv_w[0:32 * SLOTS, 3 * g + dx + 1, :],
                                                    x_slot[0:32 * SLOTS, g, rows * n:rows * (n + 1), x0 + dx:x1 + dx],
                                                    start=(t == 0), stop=(t == 2), tile_position=(0, 32 * g))
                mmul.then_inc(pe_sconv, 1)

            def shared_pointwise(k, lap):
                ps = mm[plan[("spw", k, 0)][0]]
                pe.wait_ge(*drained(("spw", k, 0), lap))
                pe.wait_ge(act_h2s, due(act_h2s, k + 1, lap))
                for n in range(2):
                    mmul = nc.tensor.matmul(ps[:, HALF * n:HALF * (n + 1)], stat[:, S_SPW:S_SPW + P],
                                            h2s[:, HALF * n:HALF * (n + 1)], start=True, stop=True)
                mmul.then_inc(pe_spw, 1)

            def proj(k, lap):
                par = (k // CHUNKS) % 2
                ps = mm[plan[("proj", k, 0)][0]]
                pe.wait_ge(*drained(("proj", k, 0), lap))
                pe.wait_ge(dve_gate, due(dve_gate, N_GATE * (k // CHUNKS + 1), lap))
                for b in range(BLOCKS):
                    pe.wait_ge(act_h2, due(act_h2, h2s_of(k, b), lap))
                    for n in range(2):
                        mmul = nc.tensor.matmul(ps[:, HALF * n:HALF * (n + 1)],
                                                proj_w[:, par, b // 2, P * (b % 2):P * (b % 2 + 1)],
                                                h2[:, b, HALF * n:HALF * (n + 1)],
                                                start=(b == 0), stop=(b == BLOCKS - 1))
                mmul.then_inc(pe_proj, 1)

            def final(k, m, lap):
                ps = mm[plan[("final", k, m)][0]]
                pe.wait_ge(*drained(("final", k, m), lap))
                pe.wait_ge(act_outs, due(act_outs, k + 1, lap))
                pe.wait_ge(dve_outd, due(dve_outd, k + 1, lap))
                for half, src in enumerate((out_s, out_d)):
                    for n in range(2):
                        mmul = nc.tensor.matmul(ps[:, HALF * n:HALF * (n + 1)], pw_s[:, half, P * m:P * (m + 1)],
                                                src[:, HALF * n:HALF * (n + 1)], start=(half == 0), stop=(half == 1))
                mmul.then_inc(pe_final, 1)

            def router_first(i_static, lap):
                ps = mm[plan[("gate1", i_static - 1, 0)][0]]
                if i_static >= 1:
                    pe.wait_ge(*drained(("gate1", i_static - 1, 0), lap))
                pe.wait_ge(act_sum, due(act_sum, CHUNKS * (i_static + 1), lap))
                for c in range(CHUNKS):
                    mmul = nc.tensor.matmul(ps[0:R, 0:P], stat[:, S_RW1:S_RW1 + R], xsum[:, c:c + 1].broadcast_to([P, P]),
                                            start=(c == 0), stop=(c == CHUNKS - 1))
                mmul.then_inc(pe_gate1, 1)

            def router_second(i_static, lap):
                ps = mm[plan[("gate2", i_static - 1, 0)][0]]
                pe.wait_ge(*drained(("gate2", i_static - 1, 0), lap))
                pe.wait_ge(act_gate, due(act_gate, i_static + 1, lap))
                nc.tensor.matmul(ps[:, 0:E], gate_h[0:R, :], stat[0:R, S_RW2:S_RW2 + E],
                                 start=True, stop=True).then_inc(pe_gate2, 1)

            do = {"proj": proj, "expand": expand, "final": final, "sconv": shared_conv, "spw": shared_pointwise,
                  "gate1": lambda i, lap: router_first(i + 1, lap), "gate2": lambda i, lap: router_second(i + 1, lap)}

            def step(k, lap):
                for name, kk, n in groups_of(k):
                    if name in ("expand", "final"):
                        do[name](kk, n, lap)
                    else:
                        do[name](kk, lap)

            pe.wait_ge(stat_in, 16)
            pe.wait_ge(setup, 2)
            ps = mm[plan[("bias", 0, 0)][0]]
            for m in range(2):
                mmul = nc.tensor.matmul(ps[:, E * m:E * (m + 1)], pw_s[:, 1, P * m:P * (m + 1)], stat[:, S_B3:S_B3 + E],
                                        start=True, stop=True)
            mmul.then_inc(pe_bias, 1)
            router_first(0, None)
            router_second(0, None)
            run(pe, step, -2, STEPS + 1)


def build(nc):
    x = nc.dram_tensor("x", (B, C, H, W), F32, kind="ExternalInput").ap()
    experts = nc.dram_tensor("experts", (E, P, X_LEN), F32, kind="ExternalInput").ap()
    shared = nc.dram_tensor("shared", (P, S_LEN), F32, kind="ExternalInput").ap()
    zeros = nc.dram_tensor("zeros", (32, GROUPS, W), F32, kind="ExternalInput").ap()
    out = nc.dram_tensor("out", (B, C, H, W), F32, kind="ExternalOutput").ap()
    moe_conv_kernel(nc, x, experts, shared, zeros, out)


def pack_experts(a):
    packed = np.zeros((E, P, X_LEN), np.float32)
    packed[:, :, X_EXP:X_EXP + 256] = a["L0_conv_ew_exp"].transpose(0, 2, 1)
    proj = a["L0_conv_ew_proj"].transpose(0, 2, 1).reshape(E, 2, P, P)
    packed[:, :, X_PROJ:X_PROJ + 256] = proj.transpose(0, 2, 1, 3).reshape(E, P, 256)
    dw = a["L0_conv_ew_dw"].reshape(E, 2, P, 9)
    packed[:, :, X_DW:X_DW + 18] = dw.transpose(0, 2, 1, 3).reshape(E, P, 18)
    for col, name in ((X_S1, "e1s"), (X_B1, "e1b"), (X_S2, "e2s"), (X_B2, "e2b")):
        packed[:, :, col:col + 2] = a["L0_conv_" + name].reshape(E, 2, P).transpose(0, 2, 1)
    packed[:, :, X_S3:X_S3 + P] = a["L0_conv_e3s"][:, None, :]
    return packed


def pack_shared(a):
    packed = np.zeros((P, S_LEN), np.float32)
    packed[:, S_SPW:S_SPW + P] = a["L0_conv_sw_pw"].T
    packed[:, S_PW:S_PW + 512] = a["L0_conv_pw"].T.reshape(2, P, C).transpose(1, 0, 2).reshape(P, 512)
    packed[:, S_BNS:S_BNS + C] = a["L0_conv_bn_s"][None, :]
    packed[:, S_BNB:S_BNB + 2] = a["L0_conv_bn_b"].reshape(2, P).T
    for n, name in enumerate(("sbn1_s", "sbn1_b", "sbn2_s", "sbn2_b")):
        packed[:, S_SBN + n] = a["L0_conv_" + name]
    packed[:, S_RW1:S_RW1 + R] = a["L0_conv_rw1"].T
    packed[0:R, S_RW2:S_RW2 + E] = a["L0_conv_rw2"].T
    packed[0:R, S_RB1] = a["L0_conv_rb1"]
    packed[:, S_RB2:S_RB2 + E] = a["L0_conv_rb2"][None, :]
    packed[:, S_B3:S_B3 + E] = a["L0_conv_e3b"].T
    dw = a["L0_conv_sw_dw"].reshape(GROUPS, 32, 3, 3).transpose(2, 1, 0, 3)
    packed[0:32 * SLOTS, S_CONV:S_EYE] = dw.reshape(32 * SLOTS, GROUPS * 3)
    packed[:, S_EYE:S_EYE + 32] = np.tile(np.eye(32, dtype=np.float32), (4, 1))
    packed[:, S_TRI:S_TRI + E * E] = np.tril(np.ones((E, E), np.float32), -1).reshape(1, E * E)
    packed[:, S_IOTA:S_IOTA + E] = np.arange(E, dtype=np.float32)[None, :]
    return packed


def kernel(**inputs):
    import concourse.bacc as bacc
    from concourse.bass_utils import run_bass_kernel_spmd

    a = {n: np.asarray(v) for n, v in inputs.items()}
    arrays = {
        "x": np.ascontiguousarray(a["x"]),
        "experts": pack_experts(a),
        "shared": pack_shared(a),
        "zeros": np.zeros((32, GROUPS, W), np.float32),
    }
    nc = bacc.Bacc("TRN2", target_bir_lowering=False, num_devices=1)
    build(nc)
    r = run_bass_kernel_spmd(nc, [arrays], core_ids=[0])
    return r.results[0]["out"]
```

```python
from contextlib import ExitStack

import numpy as np

import concourse.bass as bass
from concourse import mybir

F32 = mybir.dt.float32
BF16 = mybir.dt.bfloat16
I32 = mybir.dt.int32
ALU = mybir.AluOpType
ACT = mybir.ActivationFunctionType
AX_X = mybir.AxisListType.X

P = 128
B, C, H, W = 16, 256, 64, 64
E, K, R = 4, 2, 16
CHUNKS = 4
ROWS = H // CHUNKS
PX = ROWS * W
HALF = PX // 2
BLOCKS = 4
STEPS = B * CHUNKS
PAIR = 2 * CHUNKS
SLOTS = 3
GROUPS = P // 32

X_EXP = 0
X_PROJ = X_EXP + 256
X_DW = X_PROJ + 256
X_S1, X_B1 = X_DW + 18, X_DW + 20
X_S2, X_B2 = X_DW + 22, X_DW + 24
X_S3 = X_DW + 26
X_LEN = X_S3 + 128

S_SPW = 0
S_PW = S_SPW + 128
S_BNS = S_PW + 512
S_BNB = S_BNS + 256
S_SBN = S_BNB + 2
S_RW1 = S_SBN + 4
S_RW2 = S_RW1 + R
S_RB1 = S_RW2 + E * R
S_RB2 = S_RB1 + R
S_B3 = S_RB2 + E
S_CONV = S_B3 + E
S_EYE = S_CONV + GROUPS * 3
S_TRI = S_EYE + 32
S_IOTA = S_TRI + E * E
S_LEN = S_IOTA + E

POOL_TAPS = [(0, 0), (0, -1), (0, 1), (-1, -1)]
FULL_BELOW = [(1, 0), (-1, 0), (-1, 1), (1, -1), (1, 1)]
FULL_ABOVE = [(-1, 0), (1, 0), (-1, 1), (1, -1), (1, 1)]
NP, NV = len(POOL_TAPS), len(FULL_BELOW)


def vector_taps(c):
    return FULL_ABOVE if c == CHUNKS - 1 else FULL_BELOW


def tap_index(dy, dx):
    return 3 * (dy + 1) + dx + 1


def region(c, dy, dx):
    r0, r1 = max(ROWS * c, -dy), min(ROWS * (c + 1), H - dy)
    x0, x1 = max(0, -dx), W - max(0, dx)
    return r0, r1, x0, x1


def router_step(k):
    return k % CHUNKS == 1 and 0 < k < STEPS - CHUNKS


def plan_psum():
    order = [("bias", 0, 0), ("router", -1, 0), *PE_START]
    for k in range(STEPS + 1):
        order += groups_of(k)
    return {g: (n % 2, order[n - 2] if n >= 2 else None) for n, g in enumerate(order)}


PE_ORDER = ("proj", "expand0", "final0", "expand1", "expand2", "sconv", "final1", "expand3", "spw")
PE_ROUTER_ORDER = ("proj", "expand0", "router", "final0", "expand1", "expand2", "sconv", "final1", "expand3", "spw")
ACT_ORDER = ("prod20", "prod21", "last_shared_out", "last_expert3", "prod22", "sum", "prod23", "prod30", "expand0",
             "prod31", "prod32", "expert0", "prod33", "expand1", "next00", "next01", "next02", "expand2", "expert1",
             "next03", "next10", "shared_hidden", "next11", "next12", "expert2", "expand3", "next13")
ACT_ROUTER_ORDER = ("last_shared_out", "prod20", "last_expert3", "prod21", "prod22", "sum", "prod23", "expand0",
                    "prod30", "expert0", "prod31", "prod32", "prod33", "hidden", "expand1", "next00", "next01",
                    "next02", "expand2", "next03", "expert1", "shared_hidden", "expert2", "next10", "next11",
                    "next12", "expand3", "next13")
ACT_LAST_ORDER = ("last_shared_out", "prod20", "prod21", "last_expert3", "prod22", "prod23", "shared_hidden",
                  "prod30", "prod31", "expert0", "prod32", "prod33", "expert1", "expert2")
PE_START = (("sconv", 0, 0), ("expand", 0, 0), ("expand", 0, 1), ("expand", 0, 2), ("expand", 0, 3), ("expand", 1, 0),
            ("expand", 1, 1), ("expand", 1, 2), ("expand", 1, 3), ("spw", 0, 0))
PE_LAST_ORDER = ("sconv", "proj", "final0", "final1", "spw")
DVE_ORDER = ("tap00", "last33", "tap01", "last34", "tap02", "tap03", "tap10", "proj", "tap11", "tap04", "tap12",
             "final0", "tap20", "tap13", "tap21", "tap14", "tap22", "tap23", "tap30", "tap31", "tap24", "final1",
             "tap32")
DVE_ROUTER_ORDER = ("tap00", "last33", "last34", "tap01", "tap02", "tap03", "tap10", "proj", "tap04", "tap11",
                    "tap12", "tap20", "final0", "tap21", "tap13", "tap22", "tap14", "tap23", "tap24", "tap30",
                    "tap31", "final1", "tap32")
DVE_LAST_ORDER = ("tap00", "last33", "tap01", "last34", "tap02", "tap03", "tap10", "tap11", "tap04", "tap12", "tap13",
                  "proj", "tap20", "tap21", "tap14", "final0", "tap22", "tap30", "tap23", "final1", "tap31", "tap32",
                  "tap24")
CHOOSE_PLACES = (7, 11)
GATES_PLACE = 4


def order_of(k, usual, router, last):
    return last if k == STEPS - 1 else router if router_step(k) else usual


def groups_of(k):
    prev, cur, nxt = 1 <= k, 1 <= k < STEPS, k + 2 < STEPS
    out = []
    for item in order_of(k, PE_ORDER, PE_ROUTER_ORDER, PE_LAST_ORDER):
        name, n = item.rstrip("0123"), int(item[-1]) if item[-1].isdigit() else 0
        if name in ("proj", "final") and prev:
            out.append((name, k - 1, n))
        elif name == "expand" and nxt:
            out.append((name, k + 2, n))
        elif name in ("sconv", "spw") and cur:
            out.append((name, k, n))
        elif name == "router":
            out.append((name, k // CHUNKS, n))
    return out


def moe_conv_kernel(nc, x, experts, shared, zeros, out):
    with ExitStack() as ctx:
        def sb(name, shape, dt=F32):
            return ctx.enter_context(nc.sbuf_tensor(name, [P, *shape], dt))

        def sem(name):
            return ctx.enter_context(nc.semaphore(name))

        x_d = sb("x_d", [2, H, W])
        x_res = sb("x_res", [2, ROWS, W])
        x_slot = sb("x_slot", [GROUPS, ROWS, W])
        h = sb("h", [BLOCKS, H, W])
        part_sum = sb("part_sum", [BLOCKS, ROWS, W])
        prod = sb("prod", [NP - 1, ROWS, W])
        h2 = sb("h2", [BLOCKS, PX])
        h2s = sb("h2s", [PX])
        out_s = sb("out_s", [PX])
        out_d = sb("out_d", [PX])
        sel = sb("sel", [2, K, X_LEN])
        proj_w = sb("proj_w", [2, K, 256])
        stat = sb("stat", [S_LEN])
        conv_w = sb("conv_w", [GROUPS * 3, 32])
        pw_s = sb("pw_s", [2, 256])
        b3_out = sb("b3_out", [2, E])
        junk = sb("junk", [PX], BF16)
        warm = sb("warm", [1])
        xsum = sb("xsum", [CHUNKS])
        pre = sb("pre", [R])
        hid = sb("hid", [R])
        logit_terms = sb("logit_terms", [E, R])
        logit_sum = sb("logit_sum", [E])
        logit = sb("logit", [E])
        lmax = sb("lmax", [1])
        zed = sb("zed", [E])
        zsilu = sb("zsilu", [E])
        above = sb("above", [E, E])
        equal = sb("equal", [E, E])
        rank = sb("rank", [E])
        rank_hit = sb("rank_hit", [E])
        idx_f = sb("idx_f", [K])
        idx = sb("idx", [K], I32)
        den = sb("den", [E])
        prob = sb("prob", [E])
        psumz = sb("psumz", [1])
        gate = sb("gate", [2, K])
        gate_all = sb("gate_all", [E])
        gate_sum = sb("gate_sum", [2, 1])
        fb_terms = sb("fb_terms", [2, E])
        fb_sum = sb("fb_sum", [2])
        fbias = sb("fbias", [2, 2])

        acc = [ctx.enter_context(nc.psum_tensor(f"acc{s}", [P, ROWS, W], F32)) for s in range(2)]
        mm = [ctx.enter_context(nc.psum_tensor(f"mm{s}", [P, PX], F32)) for s in range(2)]

        rate = {}

        def counter(name, per_pair):
            s = sem(name)
            rate[s.name] = per_pair
            return s

        stat_in = sem("stat_in")
        sp_passed = sem("sp_passed")
        setup = sem("setup")
        pe_bias = sem("pe_bias")
        act_warm = sem("act_warm")
        xd_in = [[counter(f"xd_in{p}{c}", 16) for c in range(CHUNKS)] for p in range(2)]
        xres_in = [counter(f"xres_in{s}", 16 * PAIR // 2) for s in range(2)]
        xslot_in = counter("xslot_in", 16 * 14 * 2)
        sel_in = [counter(f"sel_in{p}", 16 * K) for p in range(2)]
        st_d = [[counter(f"st_d{p}{c}", 16) for c in range(CHUNKS)] for p in range(2)]
        st_s = [counter(f"st_s{s}", 16 * PAIR // 2) for s in range(2)]
        pe_expand = counter("pe_expand", BLOCKS * PAIR)
        pe_sconv = counter("pe_sconv", PAIR)
        pe_spw = counter("pe_spw", PAIR)
        pe_proj = counter("pe_proj", PAIR)
        pe_final = counter("pe_final", 2 * PAIR)
        pe_router = counter("pe_router", 2)
        act_h = counter("act_h", BLOCKS * PAIR)
        act_prod = counter("act_prod", NP * BLOCKS * PAIR)
        act_h2 = counter("act_h2", BLOCKS * PAIR)
        act_h2s = counter("act_h2s", PAIR)
        act_outs = counter("act_outs", PAIR)
        act_sum = counter("act_sum", CHUNKS * 2)
        act_hid = counter("act_hid", 2)
        act_zsilu = counter("act_zsilu", 2)
        pool_add = counter("pool_add", (NP - 1) * BLOCKS * PAIR)
        dve_tap = [counter(f"dve_tap{s}", NV * BLOCKS // 2 * PAIR) for s in range(2)]
        dve_outd = counter("dve_outd", PAIR)
        dve_out = counter("dve_out", 2 * PAIR)
        N_CHOOSE, N_GATE = 14, 13
        dve_choose = counter("dve_choose", 2 * N_CHOOSE)
        dve_gate = counter("dve_gate", 2 * N_GATE)

        def due(s, value, lap):
            return value if lap is None else lap * rate[s.name] + value

        def image(k, lap):
            i = k // CHUNKS
            return i if lap is None else i + 2 * lap

        def run(eng, step, first, last):
            for k in range(first, PAIR):
                step(k, None)
            with eng.Fori(0, STEPS // PAIR - 2) as lap:
                for k in range(PAIR, 2 * PAIR):
                    step(k, lap)
            for k in range(STEPS - PAIR, last):
                step(k, None)

        def expands(k, b): return BLOCKS * k + b + 1
        def prods(k, b, n): return NP * (BLOCKS * k + b) + n + 1
        def adds(k, b, n): return (NP - 1) * (BLOCKS * k + b) + n + 1
        def h2s_of(k, b): return BLOCKS * k + b + 1
        def taps(k, b, t): return NV * (2 * k + b // 2) + t + 1
        def finals(k, m): return 2 * k + m + 1
        def xd_loads(k): return 16 * (k // PAIR + 1)
        def xres_loads(k): return 16 * (k // 2 + 1)
        def xslot_loads(k): return 16 * (14 * (k // CHUNKS) + (4, 7, 10, 14)[k % CHUNKS])

        plan = plan_psum()
        drain = {
            "bias": lambda k, n: (setup, 3),
            "router": lambda k, n: (dve_choose, N_CHOOSE * (k + 1) + 1),
            "proj": lambda k, n: (dve_outd, k + 1),
            "final": lambda k, n: (dve_out, finals(k, n)),
            "expand": lambda k, n: (act_h, expands(k, n)),
            "sconv": lambda k, n: (act_h2s, k + 1),
            "spw": lambda k, n: (act_outs, k + 1),
        }

        def weights(par, slot, col, n=1):
            return sel[:, par, slot, col:col + n]

        block = ctx.enter_context(nc.Block())

        @block.sync
        def _(sp):
            def load_xd(i_static, c, i):
                sp.dma_start(x_d[:, i_static % 2, ROWS * c:ROWS * (c + 1), :],
                             x[i, P:, ROWS * c:ROWS * (c + 1), :]).then_inc(xd_in[i_static % 2][c], 16)

            def load_res(k, lap):
                c = k % CHUNKS
                sp.dma_start(x_res[:, k % 2], x[image(k, lap), 0:P, ROWS * c:ROWS * (c + 1), :]
                             ).then_inc(xres_in[k % 2], 16)

            def load_slots(k, lap):
                c, i = k % CHUNKS, image(k, lap)
                src = x[i, 0:P].rearrange("(g c) y w -> c g y w", g=GROUPS)
                for j in range(SLOTS):
                    r0, r1, _, _ = region(c, j - 1, 0)
                    part = x_slot[32 * j:32 * (j + 1)]
                    sp.dma_start(part[:, :, r0 - ROWS * c:r1 - ROWS * c, :], src[:, :, r0 + j - 1:r1 + j - 1, :]
                                 ).then_inc(xslot_in, 16)
                    if r1 - r0 < ROWS:
                        edge = 0 if j == 0 else ROWS - 1
                        sp.dma_start(part[:, :, edge, :], zeros).then_inc(xslot_in, 16)

            def fetch_experts(i_static, lap):
                par = i_static % 2
                sp.wait_ge(dve_choose, due(dve_choose, N_CHOOSE * (i_static + 1), lap))
                sp.sem_inc(sp_passed, 1)
                if i_static >= 2:
                    sp.wait_ge(pe_proj, due(pe_proj, CHUNKS * (i_static - 1), lap))
                    sp.sem_inc(sp_passed, 1)
                for s in range(K):
                    e = sp.value_load(idx[0:1, s:s + 1], min_val=0, max_val=E - 1)
                    sp.dma_start(sel[:, par, s, :], experts[bass.ds(e, 1), :, :].rearrange("a p l -> (a p) l")
                                 ).then_inc(sel_in[par], 16)

            def step(k, lap):
                if k % CHUNKS == 2 and router_step(k - 1):
                    fetch_experts(k // CHUNKS + 1, lap)
                c, kp = (k - 1) % CHUNKS, k - 1
                if k >= 1:
                    sp.wait_ge(dve_out, due(dve_out, finals(kp, 0), lap))
                    sp.sem_inc(sp_passed, 1)
                    sp.dma_start(out[image(kp, lap), 0:P, ROWS * c:ROWS * (c + 1), :], x_res[:, kp % 2]
                                 ).then_inc(st_s[kp % 2], 16)
                if k + 1 < STEPS:
                    sp.wait_ge(pe_sconv, due(pe_sconv, k + 1, lap))
                    sp.sem_inc(sp_passed, 1)
                    load_slots(k + 1, lap)
                if k >= 1:
                    par = (kp // CHUNKS) % 2
                    sp.wait_ge(dve_out, due(dve_out, finals(kp, 1), lap))
                    sp.sem_inc(sp_passed, 1)
                    sp.dma_start(out[image(kp, lap), P:, ROWS * c:ROWS * (c + 1), :],
                                 x_d[:, par, ROWS * c:ROWS * (c + 1), :]).then_inc(st_d[par][c], 16)
                    if k + 1 < STEPS:
                        sp.wait_ge(st_s[kp % 2], due(st_s[kp % 2], xres_loads(kp), lap))
                        sp.sem_inc(sp_passed, 1)
                        load_res(k + 1, lap)
                    if kp // CHUNKS + 2 < B:
                        sp.wait_ge(st_d[par][c], due(st_d[par][c], xd_loads(kp), lap))
                        sp.sem_inc(sp_passed, 1)
                        load_xd(kp // CHUNKS + 2, c, image(kp, lap) + 2)

            for c in range(CHUNKS):
                load_xd(0, c, 0)
                if c == 1:
                    sp.dma_start(stat[:], shared).then_inc(stat_in, 16)
            load_slots(0, None)
            fetch_experts(0, None)
            load_res(0, None)
            load_res(1, None)
            for c in range(CHUNKS):
                load_xd(1, c, 1)
            run(sp, step, 0, STEPS + 1)
            for s in range(2):
                sp.wait_ge(st_s[s], 16 * STEPS // 2)
                for c in range(CHUNKS):
                    sp.wait_ge(st_d[s][c], 16 * B // 2)

        @block.gpsimd
        def _(pool):
            def step(k, lap):
                c = k % CHUNKS
                for b in range(BLOCKS):
                    for n in range(1, NP):
                        r0, r1, x0, x1 = region(c, *POOL_TAPS[n])
                        total = part_sum[:, b, r0 - ROWS * c:r1 - ROWS * c, x0:x1]
                        pool.wait_ge(act_prod, due(act_prod, prods(k, b, n), lap))
                        if n > 1:
                            pool.wait_ge(pool_add, due(pool_add, adds(k, b, n - 2), lap))
                        nc.gpsimd.tensor_tensor(total, total, prod[:, n - 1, r0 - ROWS * c:r1 - ROWS * c, x0:x1],
                                                ALU.add).then_inc(pool_add, 1)
            run(pool, step, 0, STEPS)

        @block.scalar
        def _(act):
            def sum_x(k, lap):
                c, par = k % CHUNKS, (k // CHUNKS) % 2
                act.wait_ge(xd_in[par][c], due(xd_in[par][c], xd_loads(k), lap))
                if k >= CHUNKS:
                    act.wait_ge(pe_router, due(pe_router, k // CHUNKS, lap))
                if k >= 1:
                    act.wait_ge(act_sum, due(act_sum, k, lap))
                nc.scalar.activation(junk[:], x_d[:, par, ROWS * c:ROWS * (c + 1), :].rearrange("p y w -> p (y w)"),
                                     ACT.Copy, accum_out=xsum[:, c:c + 1]).then_inc(act_sum, 1)

            def router_hidden(i_static, lap):
                act.wait_ge(dve_choose, due(dve_choose, N_CHOOSE * i_static + 1, lap))
                if i_static >= 1:
                    act.wait_ge(dve_choose, due(dve_choose, N_CHOOSE * (i_static - 1) + 2, lap))
                nc.scalar.activation(hid[:], pre[:], ACT.Silu).then_inc(act_hid, 1)

            def router_silu(i_static, lap):
                act.wait_ge(dve_choose, due(dve_choose, N_CHOOSE * i_static + 6, lap))
                nc.scalar.activation(zsilu[:], zed[:], ACT.Silu).then_inc(act_zsilu, 1)

            def expand_out(k, b, lap):
                c, par = k % CHUNKS, (k // CHUNKS) % 2
                act.wait_ge(pe_expand, due(pe_expand, expands(k, b), lap))
                if k >= 3:
                    act.wait_ge(dve_tap[b % 2], due(dve_tap[b % 2], taps(k - 3, b, NV - 1), lap))
                nc.scalar.activation(h[:, b, ROWS * c:ROWS * (c + 1), :].rearrange("p y w -> p (y w)"),
                                     mm[plan[("expand", k, b)][0]][:], ACT.Silu,
                                     bias=weights(par, b // 2, X_B1 + b % 2), scale=weights(par, b // 2, X_S1 + b % 2)
                                     ).then_inc(act_h, 1)

            def product(k, b, n, lap):
                c, par = k % CHUNKS, (k // CHUNKS) % 2
                dy, dx = POOL_TAPS[n]
                r0, r1, x0, x1 = region(c, dy, dx)
                if n == 0:
                    act.wait_ge(act_h, due(act_h, expands(k, b), lap))
                    if k >= 1:
                        act.wait_ge(dve_tap[b % 2], due(dve_tap[b % 2], taps(k - 1, b, 0), lap))
                    dst = part_sum[:, b]
                else:
                    if k >= 1 or b >= 1:
                        act.wait_ge(pool_add, due(pool_add, adds(k, b, n - 1) - (NP - 1), lap))
                    dst = prod[:, n - 1]
                nc.scalar.activation(dst[:, r0 - ROWS * c:r1 - ROWS * c, x0:x1], h[:, b, r0 + dy:r1 + dy, x0 + dx:x1 + dx],
                                     ACT.Copy, scale=weights(par, b // 2, X_DW + 9 * (b % 2) + tap_index(dy, dx))
                                     ).then_inc(act_prod, 1)

            def expert_out(k, b, lap):
                par = (k // CHUNKS) % 2
                act.wait_ge(dve_tap[b % 2], due(dve_tap[b % 2], taps(k, b, NV - 1), lap))
                if k >= 1:
                    act.wait_ge(pe_proj, due(pe_proj, k, lap))
                nc.scalar.activation(h2[:, b, :], acc[b % 2][:].rearrange("p y w -> p (y w)"), ACT.Silu,
                                     bias=weights(par, b // 2, X_B2 + b % 2), scale=weights(par, b // 2, X_S2 + b % 2)
                                     ).then_inc(act_h2, 1)

            def shared_hidden(k, lap):
                act.wait_ge(pe_sconv, due(pe_sconv, k + 1, lap))
                if k >= 1:
                    act.wait_ge(pe_spw, due(pe_spw, k, lap))
                nc.scalar.activation(h2s[:], mm[plan[("sconv", k, 0)][0]][:], ACT.Silu,
                                     bias=stat[:, S_SBN + 1:S_SBN + 2], scale=stat[:, S_SBN:S_SBN + 1]
                                     ).then_inc(act_h2s, 1)

            def shared_out(k, lap):
                act.wait_ge(pe_spw, due(pe_spw, k + 1, lap))
                if k >= 1:
                    act.wait_ge(pe_final, due(pe_final, finals(k - 1, 1), lap))
                nc.scalar.activation(out_s[:], mm[plan[("spw", k, 0)][0]][:], ACT.Silu,
                                     bias=stat[:, S_SBN + 3:S_SBN + 4], scale=stat[:, S_SBN + 2:S_SBN + 3]
                                     ).then_inc(act_outs, 1)

            def step(k, lap):
                prev, cur, nxt, ahead = 1 <= k, k < STEPS, k + 2 < STEPS, k + 1 < STEPS
                if k % CHUNKS == 2 and router_step(k - 1):
                    router_silu(k // CHUNKS + 1, lap)
                for item in order_of(k, ACT_ORDER, ACT_ROUTER_ORDER, ACT_LAST_ORDER):
                    if item.startswith("prod") and cur:
                        product(k, int(item[4]), int(item[5]), lap)
                    elif item.startswith("next") and ahead:
                        product(k + 1, int(item[4]), int(item[5]), lap)
                    elif item.startswith("expand") and nxt:
                        expand_out(k + 2, int(item[6]), lap)
                    elif item.startswith("expert") and cur:
                        expert_out(k, int(item[6]), lap)
                    elif item == "last_expert3" and prev:
                        expert_out(k - 1, 3, lap)
                    elif item == "last_shared_out" and k >= 2:
                        shared_out(k - 1, lap)
                    elif item == "shared_hidden" and prev and cur:
                        shared_hidden(k, lap)
                    elif item == "hidden":
                        router_hidden(k // CHUNKS + 1, lap)
                    elif item == "sum":
                        if k == 0:
                            sum_x(CHUNKS, lap)
                            sum_x(CHUNKS + 1, lap)
                        if 0 <= k and k + 6 < STEPS:
                            sum_x(k + 6, lap)

            act.wait_ge(xd_in[0][0], 16)
            nc.scalar.activation(warm[:], x_d[:, 0, 0, 0:1], ACT.Silu).then_inc(act_warm, 1)
            for k in range(CHUNKS):
                sum_x(k, None)
            act.wait_ge(stat_in, 16)
            router_hidden(0, None)
            router_silu(0, None)
            act.wait_ge(sel_in[0], 16 * K)
            shared_hidden(0, None)
            expand_out(0, 0, None)
            product(0, 0, 0, None)
            product(0, 0, 1, None)
            expand_out(0, 1, None)
            expand_out(0, 2, None)
            product(0, 0, 2, None)
            product(0, 0, 3, None)
            expand_out(0, 3, None)
            expand_out(1, 0, None)
            product(0, 1, 0, None)
            product(0, 1, 1, None)
            expand_out(1, 1, None)
            expand_out(1, 2, None)
            product(0, 1, 2, None)
            product(0, 1, 3, None)
            expand_out(1, 3, None)
            shared_out(0, None)
            run(act, step, 0, STEPS + 1)

        @block.vector
        def _(dve):
            def choose(i_static, part, lap):
                done = N_CHOOSE * i_static
                by_f = logit[:].unsqueeze(1).broadcast_to([P, E, E])
                by_e = logit[:].unsqueeze(2).broadcast_to([P, E, E])
                if part == 0:
                    buf = plan[("router", i_static - 1, 0)][0]
                    dve.wait_ge(pe_router, due(pe_router, i_static + 1, lap))
                    if i_static >= 1:
                        dve.wait_ge(act_hid, due(act_hid, i_static, lap))
                    nc.vector.scalar_tensor_tensor(pre[:], mm[buf][:, 0:R], 1.0 / (H * W), stat[:, S_RB1:S_RB1 + R],
                                                   ALU.mult, ALU.add).then_inc(dve_choose, 1)
                elif part == 1:
                    dve.wait_ge(act_hid, due(act_hid, i_static + 1, lap))
                    nc.vector.tensor_tensor(logit_terms[:], stat[:, S_RW2:S_RW2 + E * R].rearrange("p (e r) -> p e r", e=E),
                                            hid[:].unsqueeze(1).broadcast_to([P, E, R]), ALU.mult).then_inc(dve_choose, 1)
                elif part == 2:
                    dve.wait_ge(dve_choose, due(dve_choose, done + 2, lap))
                    nc.vector.reduce_sum(logit_sum[:], logit_terms[:], AX_X).then_inc(dve_choose, 1)
                elif part == 3:
                    dve.wait_ge(dve_choose, due(dve_choose, done + 3, lap))
                    nc.vector.tensor_tensor(logit[:], logit_sum[:], stat[:, S_RB2:S_RB2 + E], ALU.add).then_inc(dve_choose, 1)
                elif part == 4:
                    dve.wait_ge(dve_choose, due(dve_choose, done + 4, lap))
                    nc.vector.reduce_max(lmax[:], logit[:], AX_X).then_inc(dve_choose, 1)
                elif part == 5:
                    dve.wait_ge(dve_choose, due(dve_choose, done + 5, lap))
                    if i_static >= 1:
                        dve.wait_ge(act_zsilu, due(act_zsilu, i_static, lap))
                    nc.vector.tensor_scalar(zed[:], logit[:], lmax[:], -1.0, ALU.subtract, ALU.add).then_inc(dve_choose, 1)
                    nc.vector.tensor_tensor(equal[:], by_f, by_e, ALU.is_equal).then_inc(dve_choose, 1)
                    nc.vector.tensor_tensor(above[:], by_f, by_e, ALU.is_gt).then_inc(dve_choose, 1)
                elif part == 6:
                    dve.wait_ge(dve_choose, due(dve_choose, done + 8, lap))
                    nc.vector.tensor_tensor(equal[:], equal[:], stat[:, S_TRI:S_TRI + E * E].rearrange("p (e f) -> p e f", e=E),
                                            ALU.mult).then_inc(dve_choose, 1)
                elif part == 7:
                    dve.wait_ge(dve_choose, due(dve_choose, done + 9, lap))
                    nc.vector.tensor_tensor(above[:], above[:], equal[:], ALU.add).then_inc(dve_choose, 1)
                    dve.wait_ge(dve_choose, due(dve_choose, done + 10, lap))
                    if i_static >= 1:
                        dve.wait_ge(dve_gate, due(dve_gate, N_GATE * i_static, lap))
                    nc.vector.reduce_sum(rank[:], above[:], AX_X).then_inc(dve_choose, 1)
                else:
                    s = part - 8
                    dve.wait_ge(dve_choose, due(dve_choose, done + 11 + s, lap))
                    nc.vector.scalar_tensor_tensor(rank_hit[:], rank[:], float(s), stat[:, S_IOTA:S_IOTA + E], ALU.is_equal,
                                                   ALU.mult, accum_out=idx_f[:, s:s + 1]).then_inc(dve_choose, 1)
                    if s == 1:
                        dve.wait_ge(dve_choose, due(dve_choose, done + 13, lap))
                        nc.vector.tensor_copy(idx[:], idx_f[:]).then_inc(dve_choose, 1)

            def gates(i_static, part, lap):
                done, par = N_GATE * i_static, i_static % 2
                if part == 0:
                    dve.wait_ge(act_zsilu, due(act_zsilu, i_static + 1, lap))
                    nc.vector.tensor_tensor(den[:], zed[:], zsilu[:], ALU.subtract).then_inc(dve_gate, 1)
                elif part == 1:
                    dve.wait_ge(dve_gate, due(dve_gate, done + 1, lap))
                    nc.vector.reciprocal(den[:], den[:]).then_inc(dve_gate, 1)
                elif part == 2:
                    dve.wait_ge(dve_gate, due(dve_gate, done + 2, lap))
                    nc.vector.scalar_tensor_tensor(prob[:], zsilu[:], 1.0, den[:], ALU.mult, ALU.mult,
                                                   accum_out=psumz[:]).then_inc(dve_gate, 1)
                elif part == 3:
                    dve.wait_ge(dve_gate, due(dve_gate, done + 3, lap))
                    nc.vector.reciprocal(psumz[:], psumz[:]).then_inc(dve_gate, 1)
                elif part == 4:
                    dve.wait_ge(dve_gate, due(dve_gate, done + 4, lap))
                    nc.vector.tensor_scalar(prob[:], prob[:], psumz[:], None, ALU.mult).then_inc(dve_gate, 1)
                elif part in (5, 6):
                    s = part - 5
                    dve.wait_ge(dve_gate, due(dve_gate, done + 5 + s, lap))
                    nc.vector.scalar_tensor_tensor(rank_hit[:], rank[:], float(s), prob[:], ALU.is_equal, ALU.mult,
                                                   accum_out=gate[:, par, s:s + 1]).then_inc(dve_gate, 1)
                elif part == 7:
                    nc.vector.scalar_tensor_tensor(gate_all[:], rank[:], float(K), prob[:], ALU.is_lt, ALU.mult,
                                                   accum_out=gate_sum[:, par, :]).then_inc(dve_gate, 1)
                elif part == 8:
                    dve.wait_ge(dve_gate, due(dve_gate, done + 8, lap))
                    nc.vector.tensor_tensor(fb_terms[:], b3_out[:], gate_all[:].unsqueeze(1).broadcast_to([P, 2, E]),
                                            ALU.mult).then_inc(dve_gate, 1)
                elif part == 9:
                    dve.wait_ge(dve_gate, due(dve_gate, done + 9, lap))
                    nc.vector.reduce_sum(fb_sum[:], fb_terms[:], AX_X).then_inc(dve_gate, 1)
                elif part == 10:
                    dve.wait_ge(dve_gate, due(dve_gate, done + 10, lap))
                    nc.vector.tensor_tensor(fbias[:, par, :], fb_sum[:], stat[:, S_BNB:S_BNB + 2], ALU.add).then_inc(dve_gate, 1)
                else:
                    s = part - 11
                    dve.wait_ge(sel_in[par], due(sel_in[par], 16 * K * (i_static // 2 + 1), lap))
                    if i_static >= 2:
                        dve.wait_ge(pe_proj, due(pe_proj, CHUNKS * (i_static - 1), lap))
                    nc.vector.scalar_tensor_tensor(
                        proj_w[:, par, s, :].rearrange("p (b o) -> p b o", b=2),
                        weights(par, s, X_PROJ, 256).rearrange("p (b o) -> p b o", b=2), gate[:, par, s:s + 1],
                        weights(par, s, X_S3, P).unsqueeze(1).broadcast_to([P, 2, P]),
                        ALU.mult, ALU.mult).then_inc(dve_gate, 1)

            def tap(k, b, t, lap):
                c, par = k % CHUNKS, (k // CHUNKS) % 2
                dy, dx = vector_taps(c)[t]
                r0, r1, x0, x1 = region(c, dy, dx)
                dst = acc[b % 2][:, r0 - ROWS * c:r1 - ROWS * c, x0:x1]
                if t == 0:
                    dve.wait_ge(pool_add, due(pool_add, adds(k, b, NP - 2), lap))
                    if c < CHUNKS - 1:
                        dve.wait_ge(act_h, due(act_h, expands(k + 1, b), lap))
                    if k >= 1 or b >= 2:
                        dve.wait_ge(act_h2, due(act_h2, h2s_of(k, b) - 2, lap))
                    before = part_sum[:, b]
                else:
                    dve.wait_ge(dve_tap[b % 2], due(dve_tap[b % 2], taps(k, b, t - 1), lap))
                    before = dst
                nc.vector.scalar_tensor_tensor(dst, h[:, b, r0 + dy:r1 + dy, x0 + dx:x1 + dx],
                                               weights(par, b // 2, X_DW + 9 * (b % 2) + tap_index(dy, dx)), before,
                                               ALU.mult, ALU.add).then_inc(dve_tap[b % 2], 1)

            def expert_sum(k, lap):
                c, par = k % CHUNKS, (k // CHUNKS) % 2
                dve.wait_ge(pe_proj, due(pe_proj, k + 1, lap))
                if k >= 1:
                    dve.wait_ge(pe_final, due(pe_final, finals(k - 1, 1), lap))
                dve.wait_ge(xd_in[par][c], due(xd_in[par][c], xd_loads(k), lap))
                nc.vector.scalar_tensor_tensor(out_d[:], x_d[:, par, ROWS * c:ROWS * (c + 1), :].rearrange("p y w -> p (y w)"),
                                               gate_sum[:, par, :], mm[plan[("proj", k, 0)][0]][:],
                                               ALU.mult, ALU.add).then_inc(dve_outd, 1)

            def output(k, m, lap):
                c, par = k % CHUNKS, (k // CHUNKS) % 2
                dve.wait_ge(pe_final, due(pe_final, finals(k, m), lap))
                if m == 0:
                    dve.wait_ge(xres_in[k % 2], due(xres_in[k % 2], xres_loads(k), lap))
                    place = x_res[:, k % 2].rearrange("p y w -> p (y w)")
                else:
                    dve.wait_ge(dve_outd, due(dve_outd, k + 1, lap))
                    place = x_d[:, par, ROWS * c:ROWS * (c + 1), :].rearrange("p y w -> p (y w)")
                nc.vector.scalar_tensor_tensor(place, mm[plan[("final", k, m)][0]][:], fbias[:, par, m:m + 1], place,
                                               ALU.add, ALU.add).then_inc(dve_out, 1)

            def router_part(k, place, lap):
                first, second = CHOOSE_PLACES
                if router_step(k) and place == first:
                    choose(k // CHUNKS + 1, 0, lap)
                if router_step(k) and second <= place < second + 9:
                    choose(k // CHUNKS + 1, place - second + 1, lap)
                if k % CHUNKS == 2 and router_step(k - 1) and GATES_PLACE <= place < GATES_PLACE + 13:
                    gates(k // CHUNKS + 1, place - GATES_PLACE, lap)

            def step(k, lap):
                place = 0
                for item in order_of(k, DVE_ORDER, DVE_ROUTER_ORDER, DVE_LAST_ORDER):
                    if item.startswith("tap"):
                        if k < STEPS:
                            tap(k, int(item[3]), int(item[4]), lap)
                    elif item.startswith("last"):
                        if k >= 1:
                            tap(k - 1, int(item[4]), int(item[5]), lap)
                    elif item == "proj" and k >= 1:
                        expert_sum(k - 1, lap)
                    elif item.startswith("final") and k >= 1:
                        output(k - 1, int(item[5]), lap)
                    if item.startswith(("tap", "last")):
                        router_part(k, place, lap)
                        place += 1

            dve.wait_ge(stat_in, 16)
            nc.vector.tensor_tensor(pw_s[:], stat[:, S_PW:S_PW + 512].rearrange("p (k o) -> p k o", k=2),
                                    stat[:, S_BNS:S_BNS + 256].unsqueeze(1).broadcast_to([P, 2, 256]),
                                    ALU.mult).then_inc(setup, 1)
            nc.vector.tensor_tensor(conv_w[:], stat[:, S_CONV:S_EYE].unsqueeze(2).broadcast_to([P, GROUPS * 3, 32]),
                                    stat[:, S_EYE:S_EYE + 32].unsqueeze(1).broadcast_to([P, GROUPS * 3, 32]),
                                    ALU.mult).then_inc(setup, 1)
            dve.wait_ge(pe_bias, 1)
            nc.vector.tensor_copy(b3_out[:], mm[plan[("bias", 0, 0)][0]][:, 0:2 * E].rearrange("p (m e) -> p m e", m=2)
                                  ).then_inc(setup, 1)
            dve.wait_ge(setup, 3)
            for part in range(10):
                choose(0, part, None)
            for part in range(13):
                gates(0, part, None)
            dve.wait_ge(dve_gate, N_GATE)
            run(dve, step, 0, STEPS + 1)

        @block.tensor
        def _(pe):
            def drained(group, lap):
                name, k, n = plan[group][1]
                s, value = drain[name](k, n)
                return s, due(s, value, lap)

            def expand(k, b, lap):
                c, par = k % CHUNKS, (k // CHUNKS) % 2
                ps = mm[plan[("expand", k, b)][0]]
                pe.wait_ge(*drained(("expand", k, b), lap))
                pe.wait_ge(xd_in[par][c], due(xd_in[par][c], xd_loads(k), lap))
                pe.wait_ge(sel_in[par], due(sel_in[par], 16 * K * (k // PAIR + 1), lap))
                for n in range(2):
                    mmul = nc.tensor.matmul(ps[:, HALF * n:HALF * (n + 1)],
                                            weights(par, b // 2, X_EXP + P * (b % 2), P),
                                            x_d[:, par, ROWS * c + ROWS // 2 * n:ROWS * c + ROWS // 2 * (n + 1), :],
                                            start=True, stop=True)
                mmul.then_inc(pe_expand, 1)

            def shared_conv(k, lap):
                ps = mm[plan[("sconv", k, 0)][0]]
                pe.wait_ge(*drained(("sconv", k, 0), lap))
                pe.wait_ge(xslot_in, due(xslot_in, xslot_loads(k), lap))
                rows = ROWS // 2
                for n in range(2):
                    for t, dx in enumerate((0, -1, 1)):
                        x0, x1 = max(0, -dx), W - max(0, dx)
                        for g in range(GROUPS):
                            dst = ps[32 * g:32 * (g + 1), HALF * n:HALF * (n + 1)].rearrange("p (y w) -> p y w", w=W)
                            mmul = nc.tensor.matmul(dst[:, :, x0:x1], conv_w[0:32 * SLOTS, 3 * g + dx + 1, :],
                                                    x_slot[0:32 * SLOTS, g, rows * n:rows * (n + 1), x0 + dx:x1 + dx],
                                                    start=(t == 0), stop=(t == 2), tile_position=(0, 32 * g))
                mmul.then_inc(pe_sconv, 1)

            def shared_pointwise(k, lap):
                ps = mm[plan[("spw", k, 0)][0]]
                pe.wait_ge(*drained(("spw", k, 0), lap))
                pe.wait_ge(act_h2s, due(act_h2s, k + 1, lap))
                for n in range(2):
                    mmul = nc.tensor.matmul(ps[:, HALF * n:HALF * (n + 1)], stat[:, S_SPW:S_SPW + P],
                                            h2s[:, HALF * n:HALF * (n + 1)], start=True, stop=True)
                mmul.then_inc(pe_spw, 1)

            def proj(k, lap):
                par = (k // CHUNKS) % 2
                ps = mm[plan[("proj", k, 0)][0]]
                pe.wait_ge(*drained(("proj", k, 0), lap))
                pe.wait_ge(dve_gate, due(dve_gate, N_GATE * (k // CHUNKS + 1), lap))
                for b in range(BLOCKS):
                    pe.wait_ge(act_h2, due(act_h2, h2s_of(k, b), lap))
                    for n in range(2):
                        mmul = nc.tensor.matmul(ps[:, HALF * n:HALF * (n + 1)],
                                                proj_w[:, par, b // 2, P * (b % 2):P * (b % 2 + 1)],
                                                h2[:, b, HALF * n:HALF * (n + 1)],
                                                start=(b == 0), stop=(b == BLOCKS - 1))
                mmul.then_inc(pe_proj, 1)

            def final(k, m, lap):
                ps = mm[plan[("final", k, m)][0]]
                pe.wait_ge(*drained(("final", k, m), lap))
                pe.wait_ge(act_outs, due(act_outs, k + 1, lap))
                for half, src in enumerate((out_s, out_d)):
                    if half == 1:
                        pe.wait_ge(dve_outd, due(dve_outd, k + 1, lap))
                    for n in range(2):
                        mmul = nc.tensor.matmul(ps[:, HALF * n:HALF * (n + 1)], pw_s[:, half, P * m:P * (m + 1)],
                                                src[:, HALF * n:HALF * (n + 1)], start=(half == 0), stop=(half == 1))
                mmul.then_inc(pe_final, 1)

            def router(i_static, lap):
                ps = mm[plan[("router", i_static - 1, 0)][0]]
                if i_static >= 1:
                    pe.wait_ge(*drained(("router", i_static - 1, 0), lap))
                pe.wait_ge(act_sum, due(act_sum, CHUNKS * (i_static + 1), lap))
                for c in range(CHUNKS):
                    mmul = nc.tensor.matmul(ps[:, 0:R], xsum[:, c:c + 1].broadcast_to([P, P]), stat[:, S_RW1:S_RW1 + R],
                                            start=(c == 0), stop=(c == CHUNKS - 1))
                mmul.then_inc(pe_router, 1)

            run_group = {"proj": proj, "expand": expand, "final": final, "sconv": shared_conv, "spw": shared_pointwise,
                         "router": lambda i, lap: router(i + 1, lap)}

            def groups(order, lap):
                for name, k, n in order:
                    if name in ("expand", "final"):
                        run_group[name](k, n, lap)
                    else:
                        run_group[name](k, lap)

            def step(k, lap):
                groups(groups_of(k), lap)

            pe.wait_ge(stat_in, 16)
            pe.wait_ge(setup, 2)
            ps = mm[plan[("bias", 0, 0)][0]]
            for m in range(2):
                mmul = nc.tensor.matmul(ps[:, E * m:E * (m + 1)], pw_s[:, 1, P * m:P * (m + 1)], stat[:, S_B3:S_B3 + E],
                                        start=True, stop=True)
            mmul.then_inc(pe_bias, 1)
            router(0, None)
            groups(PE_START, None)
            run(pe, step, 0, STEPS + 1)


def build(nc):
    x = nc.dram_tensor("x", (B, C, H, W), F32, kind="ExternalInput").ap()
    experts = nc.dram_tensor("experts", (E, P, X_LEN), F32, kind="ExternalInput").ap()
    shared = nc.dram_tensor("shared", (P, S_LEN), F32, kind="ExternalInput").ap()
    zeros = nc.dram_tensor("zeros", (32, GROUPS, W), F32, kind="ExternalInput").ap()
    out = nc.dram_tensor("out", (B, C, H, W), F32, kind="ExternalOutput").ap()
    moe_conv_kernel(nc, x, experts, shared, zeros, out)


def pack_experts(a):
    packed = np.zeros((E, P, X_LEN), np.float32)
    packed[:, :, X_EXP:X_EXP + 256] = a["L0_conv_ew_exp"].transpose(0, 2, 1)
    proj = a["L0_conv_ew_proj"].transpose(0, 2, 1).reshape(E, 2, P, P)
    packed[:, :, X_PROJ:X_PROJ + 256] = proj.transpose(0, 2, 1, 3).reshape(E, P, 256)
    dw = a["L0_conv_ew_dw"].reshape(E, 2, P, 9)
    packed[:, :, X_DW:X_DW + 18] = dw.transpose(0, 2, 1, 3).reshape(E, P, 18)
    for col, name in ((X_S1, "e1s"), (X_B1, "e1b"), (X_S2, "e2s"), (X_B2, "e2b")):
        packed[:, :, col:col + 2] = a["L0_conv_" + name].reshape(E, 2, P).transpose(0, 2, 1)
    packed[:, :, X_S3:X_S3 + P] = a["L0_conv_e3s"][:, None, :]
    return packed


def pack_shared(a):
    packed = np.zeros((P, S_LEN), np.float32)
    packed[:, S_SPW:S_SPW + P] = a["L0_conv_sw_pw"].T
    packed[:, S_PW:S_PW + 512] = a["L0_conv_pw"].T.reshape(2, P, C).transpose(1, 0, 2).reshape(P, 512)
    packed[:, S_BNS:S_BNS + C] = a["L0_conv_bn_s"][None, :]
    packed[:, S_BNB:S_BNB + 2] = a["L0_conv_bn_b"].reshape(2, P).T
    for n, name in enumerate(("sbn1_s", "sbn1_b", "sbn2_s", "sbn2_b")):
        packed[:, S_SBN + n] = a["L0_conv_" + name]
    packed[:, S_RW1:S_RW1 + R] = a["L0_conv_rw1"].T
    packed[:, S_RW2:S_RW2 + E * R] = a["L0_conv_rw2"].reshape(1, E * R)
    packed[:, S_RB1:S_RB1 + R] = a["L0_conv_rb1"][None, :]
    packed[:, S_RB2:S_RB2 + E] = a["L0_conv_rb2"][None, :]
    packed[:, S_B3:S_B3 + E] = a["L0_conv_e3b"].T
    dw = a["L0_conv_sw_dw"].reshape(GROUPS, 32, 3, 3).transpose(2, 1, 0, 3)
    packed[0:32 * SLOTS, S_CONV:S_EYE] = dw.reshape(32 * SLOTS, GROUPS * 3)
    packed[:, S_EYE:S_EYE + 32] = np.tile(np.eye(32, dtype=np.float32), (4, 1))
    packed[:, S_TRI:S_TRI + E * E] = np.tril(np.ones((E, E), np.float32), -1).reshape(1, E * E)
    packed[:, S_IOTA:S_IOTA + E] = np.arange(E, dtype=np.float32)[None, :]
    return packed


def kernel(**inputs):
    import concourse.bacc as bacc
    from concourse.bass_utils import run_bass_kernel_spmd

    a = {n: np.asarray(v) for n, v in inputs.items()}
    arrays = {
        "x": np.ascontiguousarray(a["x"]),
        "experts": pack_experts(a),
        "shared": pack_shared(a),
        "zeros": np.zeros((32, GROUPS, W), np.float32),
    }
    nc = bacc.Bacc("TRN2", target_bir_lowering=False, num_devices=1)
    build(nc)
    r = run_bass_kernel_spmd(nc, [arrays], core_ids=[0])
    return r.results[0]["out"]
```
